# Optimizing a Trainium2 kernel written in Bass

```python
import numpy as np
import jax
import jax.numpy as jnp

def _softmax(x, axis=-1):
    return jax.nn.softmax(x, axis=axis)

def _gelu(x):
    return jax.nn.gelu(x, approximate=True)

def _silu(x):
    return jax.nn.silu(x)

def _sigmoid(x):
    return jax.nn.sigmoid(x)

def _layernorm(x, axis=-1, eps=1e-05):
    m = jnp.mean(x, axis=axis, keepdims=True)
    v = jnp.var(x, axis=axis, keepdims=True)
    return (x - m) / jnp.sqrt(v + eps)

def _scatter_add(tgt, idx, src, axis=0):
    return tgt.at[idx].add(src)

def _segment_sum(src, seg, n):
    return jax.ops.segment_sum(src, seg, n)
kernel_name = 'mk_adj_preln_d4_adj_r2_91ec05'

def setup_inputs(seed: int=0):
    np.random.seed(seed)
    _w = jnp.asarray

    def _rec_inputs():
        import jax
        import jax.numpy as jnp
        _gk = jax.random.key(seed)
        x = -0.0005207 + 1.001 * jax.random.normal(jax.random.fold_in(_gk, 1), (4096, 128), jnp.float32)
        _a = jax.random.bernoulli(jax.random.fold_in(_gk, 2), 0.00195312, (4096, 4096))
        _a = jnp.logical_or(_a, jnp.eye(4096, dtype=bool))
        _af = _a.astype(jnp.float32)
        _af = _af * jax.random.uniform(jax.random.fold_in(_gk, 3), (4096, 4096), jnp.float32, 0.05, 1)
        adj = _af
        return (x, adj)
    x, adj = _rec_inputs()

    def _L0_gnn_setup():
        import jax, jax.numpy as jnp
        import numpy as np
        import math
        N = 4096
        FIN = 128
        FOUT = 128
        key = jax.random.key(seed)
        k1, k2, k3, k4 = jax.random.split(key, 4)
        x = jax.random.normal(k1, (N, FIN), dtype=jnp.float32)
        adj = jax.random.uniform(k2, (N, N), dtype=jnp.float32)
        stdv = 1.0 / math.sqrt(FOUT)
        W = jax.random.uniform(k3, (FIN, FOUT), minval=-stdv, maxval=stdv, dtype=jnp.float32)
        b = jax.random.uniform(k4, (FOUT,), minval=-stdv, maxval=stdv, dtype=jnp.float32)
        return {'input': x, 'adj': adj, 'W': W, 'b': b}
    _L0_gnn_all = _L0_gnn_setup()
    _L0_gnn_in = {k: v for k, v in _L0_gnn_all.items() if k in ('W', 'b')}
    del _L0_gnn_all

    def _L1_gnn_setup():
        import jax, jax.numpy as jnp
        import numpy as np
        MIN_NORM = 1e-15
        BALL_EPS = 1e-05
        C_IN = 1.0
        C_OUT = 1.0

        def _artanh(x):
            x = jnp.clip(x, -1.0 + 1e-07, 1.0 - 1e-07)
            return 0.5 * (jnp.log1p(x) - jnp.log1p(-x))

        def _norm(x):
            return jnp.maximum(jnp.linalg.norm(x, axis=-1, keepdims=True), MIN_NORM)

        def proj(x, c):
            norm = _norm(x)
            maxnorm = (1.0 - BALL_EPS) / jnp.sqrt(c)
            return jnp.where(norm > maxnorm, x / norm * maxnorm, x)

        def expmap0(u, c):
            sc = jnp.sqrt(c)
            un = _norm(u)
            return jnp.tanh(sc * un) * u / (sc * un)

        def logmap0(p, c):
            sc = jnp.sqrt(c)
            pn = _norm(p)
            return _artanh(sc * pn) * p / (sc * pn)

        def mobius_matvec(m, x, c):
            sc = jnp.sqrt(c)
            xn = _norm(x)
            mx = x @ m.T
            mxn = _norm(mx)
            res = jnp.tanh(mxn / xn * _artanh(sc * xn)) * mx / (mxn * sc)
            zero_row = jnp.all(mx == 0, axis=-1, keepdims=True)
            return jnp.where(zero_row, jnp.zeros((), dtype=res.dtype), res)

        def mobius_add(x, y, c):
            x2 = jnp.sum(x * x, axis=-1, keepdims=True)
            y2 = jnp.sum(y * y, axis=-1, keepdims=True)
            xy = jnp.sum(x * y, axis=-1, keepdims=True)
            num = (1.0 + 2.0 * c * xy + c * y2) * x + (1.0 - c * x2) * y
            denom = 1.0 + 2.0 * c * xy + c * c * x2 * y2
            return num / jnp.maximum(denom, MIN_NORM)
        key = jax.random.key(seed)
        k1, k2, k3, k4 = jax.random.split(key, 4)
        N, D_IN, D_OUT = (4096, 128, 128)
        x = proj(0.05 * jax.random.normal(k1, (N, D_IN), dtype=jnp.float32), C_IN)
        adj = jax.random.uniform(k2, (N, N), dtype=jnp.float32)
        adj = adj / jnp.sum(adj, axis=1, keepdims=True)
        bound = np.sqrt(2.0) * np.sqrt(6.0 / (D_IN + D_OUT))
        weight = jax.random.uniform(k3, (D_OUT, D_IN), dtype=jnp.float32, minval=-bound, maxval=bound)
        bias = 0.01 * jax.random.normal(k4, (D_OUT,), dtype=jnp.float32)
        return {'x': x, 'adj': adj, 'weight': weight, 'bias': bias}
    _L1_gnn_all = _L1_gnn_setup()
    _L1_gnn_in = {k: v for k, v in _L1_gnn_all.items() if k in ('weight', 'bias')}
    del _L1_gnn_all

    def _L2_gnn_setup():
        import jax, jax.numpy as jnp
        import numpy as np
        N = 4096
        IN_F = 128
        OUT_F = 128
        key = jax.random.key(seed)
        kx, ka, kw, kb = jax.random.split(key, 4)
        X = jax.random.uniform(kx, (N, IN_F), dtype=jnp.float32)
        A = jax.random.uniform(ka, (N, N), dtype=jnp.float32)
        bound = 1.0 / np.sqrt(IN_F)
        W = jax.random.uniform(kw, (OUT_F, IN_F), minval=-bound, maxval=bound, dtype=jnp.float32)
        b = jax.random.uniform(kb, (OUT_F,), minval=-bound, maxval=bound, dtype=jnp.float32)
        return {'X': X, 'A': A, 'W': W, 'b': b}
    _L2_gnn_all = _L2_gnn_setup()
    _L2_gnn_in = {k: v for k, v in _L2_gnn_all.items() if k in ('W', 'b')}
    del _L2_gnn_all

    def _L3_gnn_setup():
        import jax, jax.numpy as jnp
        import numpy as np
        N = 8192
        IN_DIM = 128
        OUT_DIM = 128
        key = jax.random.key(seed)
        k1, k2, k3 = jax.random.split(key, 3)
        X = jax.random.normal(k1, (N, IN_DIM), dtype=jnp.float32)
        adjm = jax.random.uniform(k2, (N, N), dtype=jnp.float32)
        stdv = np.sqrt(2.0 / (IN_DIM + OUT_DIM))
        weights = jax.random.uniform(k3, (IN_DIM, OUT_DIM), dtype=jnp.float32, minval=-stdv, maxval=stdv)
        return {'X': X, 'adjm': adjm, 'weights': weights}
    _L3_gnn_all = _L3_gnn_setup()
    _L3_gnn_in = {k: v for k, v in _L3_gnn_all.items() if k in ('weights',)}
    del _L3_gnn_all
    return {'x': x, 'adj': adj, 'L0_gnn_W': _L0_gnn_in['W'], 'L0_gnn_b': _L0_gnn_in['b'], 'L1_gnn_weight': _L1_gnn_in['weight'], 'L1_gnn_bias': _L1_gnn_in['bias'], 'L2_gnn_W': _L2_gnn_in['W'], 'L2_gnn_b': _L2_gnn_in['b'], 'L3_gnn_weights': _L3_gnn_in['weights']}

def reference(x, adj, L0_gnn_W, L0_gnn_b, L1_gnn_weight, L1_gnn_bias, L2_gnn_W, L2_gnn_b, L3_gnn_weights):
    import jax
    import jax.numpy as jnp

    def _L0_gnn_ref(input, adj, W, b):
        import jax, jax.numpy as jnp
        import numpy as np
        import math
        N = 4096
        FIN = 128
        FOUT = 128
        A = adj + jnp.eye(adj.shape[0], dtype=adj.dtype)
        D = 1.0 / jnp.sqrt(jnp.sum(A, axis=1))
        A = A * D[:, None] * D[None, :]
        support = input @ W
        out = A @ support
        return jax.nn.relu(out + b)

    def _L1_gnn_ref(x, adj, weight, bias):
        import jax, jax.numpy as jnp
        import numpy as np
        MIN_NORM = 1e-15
        BALL_EPS = 1e-05
        C_IN = 1.0
        C_OUT = 1.0

        def _artanh(x):
            x = jnp.clip(x, -1.0 + 1e-07, 1.0 - 1e-07)
            return 0.5 * (jnp.log1p(x) - jnp.log1p(-x))

        def _norm(x):
            return jnp.maximum(jnp.linalg.norm(x, axis=-1, keepdims=True), MIN_NORM)

        def proj(x, c):
            norm = _norm(x)
            maxnorm = (1.0 - BALL_EPS) / jnp.sqrt(c)
            return jnp.where(norm > maxnorm, x / norm * maxnorm, x)

        def expmap0(u, c):
            sc = jnp.sqrt(c)
            un = _norm(u)
            return jnp.tanh(sc * un) * u / (sc * un)

        def logmap0(p, c):
            sc = jnp.sqrt(c)
            pn = _norm(p)
            return _artanh(sc * pn) * p / (sc * pn)

        def mobius_matvec(m, x, c):
            sc = jnp.sqrt(c)
            xn = _norm(x)
            mx = x @ m.T
            mxn = _norm(mx)
            res = jnp.tanh(mxn / xn * _artanh(sc * xn)) * mx / (mxn * sc)
            zero_row = jnp.all(mx == 0, axis=-1, keepdims=True)
            return jnp.where(zero_row, jnp.zeros((), dtype=res.dtype), res)

        def mobius_add(x, y, c):
            x2 = jnp.sum(x * x, axis=-1, keepdims=True)
            y2 = jnp.sum(y * y, axis=-1, keepdims=True)
            xy = jnp.sum(x * y, axis=-1, keepdims=True)
            num = (1.0 + 2.0 * c * xy + c * y2) * x + (1.0 - c * x2) * y
            denom = 1.0 + 2.0 * c * xy + c * c * x2 * y2
            return num / jnp.maximum(denom, MIN_NORM)
        h = proj(mobius_matvec(weight, x, C_IN), C_IN)
        hyp_bias = proj(expmap0(bias[None, :], C_IN), C_IN)
        h = proj(mobius_add(h, hyp_bias, C_IN), C_IN)
        x_tangent = logmap0(h, C_IN)
        support_t = adj @ x_tangent
        h = proj(expmap0(support_t, C_IN), C_IN)
        xt = jax.nn.relu(logmap0(h, C_IN))
        return proj(expmap0(xt, C_OUT), C_OUT)

    def _L2_gnn_ref(X, A, W, b):
        import jax, jax.numpy as jnp
        import numpy as np
        N = 4096
        IN_F = 128
        OUT_F = 128
        n = A.shape[0]
        A_hat = A + jnp.eye(n, dtype=A.dtype)
        deg = jnp.sum(A_hat, axis=1)
        d_inv_sqrt = 1.0 / jnp.sqrt(deg)
        A_norm = A_hat * d_inv_sqrt[:, None] * d_inv_sqrt[None, :]
        h = A_norm @ X
        out = h @ W.T + b
        return out

    def _L3_gnn_ref(X, adjm, weights):
        import jax, jax.numpy as jnp
        import numpy as np
        N = 8192
        IN_DIM = 128
        OUT_DIM = 128
        XW = X @ weights
        Y = adjm @ XW
        return jax.nn.relu(Y)
    h = jnp.maximum(_layernorm(x, axis=-1), 0.0)
    x = x + _L0_gnn_ref(h, adj, L0_gnn_W, L0_gnn_b)
    h = jnp.maximum(_layernorm(x, axis=-1), 0.0)
    x = x + _L1_gnn_ref(h, adj, L1_gnn_weight, L1_gnn_bias)
    h = jnp.maximum(_layernorm(x, axis=-1), 0.0)
    x = x + _L2_gnn_ref(h, adj, L2_gnn_W, L2_gnn_b)
    h = jnp.maximum(_layernorm(x, axis=-1), 0.0)
    x = x + _L3_gnn_ref(h, adj, L3_gnn_weights)
    return x

_drawn_inputs = setup_inputs


def setup_inputs(seed=0):
    import zlib

    import numpy as np

    out = dict(_drawn_inputs(seed))
    spreads = {}
    factors = {}
    for name, (base, spread) in spreads.items():
        noise = np.random.default_rng([zlib.crc32(name.encode()), seed]).standard_normal(out[name].shape)
        drawn = base * np.exp(spread * noise) if base else spread * noise
        out[name] = jnp.asarray(drawn.astype(out[name].dtype))
    for name, factor in factors.items():
        out[name] = (out[name] * factor).astype(out[name].dtype)
    return out
```

```python
import concourse.bass as bass
from concourse import mybir
from contextlib import ExitStack

FP32 = mybir.dt.float32
FP32R = mybir.dt.float32r
ALU = mybir.AluOpType
ACT = mybir.ActivationFunctionType

N = 4096
F = 128
P = 128
LAYERS = 4
SLAB = 512
SLABS = N // SLAB
TILES = SLAB // P
CHUNKS = N // SLAB
UNIT = 2 * SLAB
LAST = CHUNKS - 1
RING = 7
SPLIT = 4
RING_PER_SLAB = 2 * LAST
UNITS_PER_SLAB = 2 * CHUNKS

LN_EPS = 1e-5
TINY = 1e-15
TINY2 = TINY * TINY
MAXNORM = 1.0 - 1e-5
CLIP = 1.0 - 1e-7
ATANH_MAX = 6.1030338227611125
SERIES_BELOW = 0.25
SERIES = [1.0 / 11, 1.0 / 9, 1.0 / 7, 1.0 / 5, 1.0 / 3, 1.0]


def ring_order():
    units = []
    for i in range(SLABS):
        cs = list(range(i + 1, LAST)) + list(range(min(i, LAST)))
        units += [(i, c, h) for c in cs for h in range(2)]
    for i in range(SLABS - 3, -1, -1):
        units += [(i, c, h) for c in range(LAST - 1, i, -1) for h in range(2)]
    return units


def split_order():
    units = []
    for i in range(SLABS):
        if i:
            units += [(i - 1, i - 1, h) for h in range(2)]
        units += [(i, c, h) for c in range(i) for h in range(2)]
    units += [(LAST, LAST, h) for h in range(2)]
    for i in range(SLABS - 2, -1, -1):
        units += [(i, c, h) for c in range(LAST, i, -1) for h in range(2)]
    return units


RING0 = ring_order()
SPLIT0 = split_order()
PASS1_RING = 2 * (6 * (SLABS - 1) + LAST)
PASS1_SPLIT = 2 * (SLABS * (SLABS - 1) // 2 + SLABS)
EVACS0 = 2 * SLABS - 1


def row_steps():
    done, count = {}, 0
    for i in range(SLABS):
        fresh = True
        own = [(i, c, h) for c in list(range(i + 1, LAST)) + [LAST] + ([i] if i < LAST else []) for h in range(2)]
        for unit in own:
            if i == 0 and unit == own[-1]:
                count += 1
                continue
            count += 1 if fresh else 2
            fresh = False
            done[unit] = count
    return done


ROW_STEPS = row_steps()


def split_index(layer, slab, u):
    return layer * SLABS * UNITS_PER_SLAB + slab * UNITS_PER_SLAB + u


def ring_laps(layer, slab):
    return len(RING0) // RING + (layer - 1) * SLABS * RING_PER_SLAB // RING + slab * (RING_PER_SLAB // RING)


def evac_index(layer, slab):
    return EVACS0 + (layer - 1) * SLABS + slab


def slab0_chunks(layer):
    return list(range(LAST, -1, -1)) if layer == 1 else list(range(CHUNKS))


def place(layer, slab):
    return LAST - slab if layer == 1 else slab


def build(nc, adj, x_in, w_in, bias_in, out):
    ctx = ExitStack()
    with ctx:
        def sb(name, shape, dt=FP32):
            return ctx.enter_context(nc.sbuf_tensor(name, shape, dt))

        def pb(name, shape):
            return ctx.enter_context(nc.psum_tensor(name, shape, FP32))

        def sem(name):
            return ctx.enter_context(nc.semaphore(name))

        raw = sb("raw", [P, RING, UNIT])
        res = sb("res", [P, SLABS, 2 * UNIT])
        diag = sb("diag", [P, 2 * UNIT])
        hi = sb("hi", [P, SPLIT, UNIT], FP32R)
        lo = sb("lo", [P, SPLIT, UNIT], FP32R)
        x = sb("x", [P, N // P, F])
        s_next = sb("s_next", [P, N // P, F])
        s_hi = sb("s_hi", [P, N // P, F], FP32R)
        s_lo = sb("s_lo", [P, N // P, F], FP32R)
        w = sb("w", [P, LAYERS, F])
        bias = sb("bias", [P, 3, F])
        hyp_b = sb("hyp_b", [P, 1, F])
        o_sb = sb("o_sb", [P, SLAB])
        h = sb("h", [P, TILES, F])
        hT = sb("hT", [P, SLAB])
        row_part = sb("row_part", [P, SLAB])
        ident = sb("ident", [P, P])
        ident_r = sb("ident_r", [P, P], FP32R)
        ones = sb("ones", [P, P])
        mean_r = sb("mean_r", [P, P], FP32R)
        scale_d = sb("scale_d", [P, N // P])
        deg1 = sb("deg1", [P, TILES])
        minus_half = sb("minus_half", [P, 2 * TILES])
        half = sb("half", [P, 2 * TILES])
        stats = sb("stats", [P, TILES, 6])
        mv = sb("mv", [P, TILES, 2])
        var_eps = sb("var_eps", [P, TILES])
        rstd = sb("rstd", [P, TILES])
        ln_scale = sb("ln_scale", [P, TILES])
        ln_bias = sb("ln_bias", [P, TILES])
        spare = sb("spare", [P, 1])
        junk_a = sb("junk_a", [P, 2 * TILES, F])
        junk_v = sb("junk_v", [P, TILES, F])
        sq = sb("sq", [P, 2 * TILES])
        nrm = sb("nrm", [P, 2 * TILES])
        hyp = sb("hyp", [P, 32, TILES])
        bstat = sb("bstat", [P, 16])

        acc = [pb(f"acc{b}", [P, SLAB]) for b in range(2)]
        row_ps = pb("row_ps", [P, SLAB])
        deg_ps = pb("deg_ps", [P, TILES])
        o_ps = pb("o_ps", [P, TILES, P])
        h_ps = pb("h_ps", [P, SLAB])
        m_ps = pb("m_ps", [P, TILES, F])

        raw_landed = [sem(f"raw_landed{n}") for n in range(RING)]
        res_landed = sem("res_landed")
        diag_landed = sem("diag_landed")
        consts_landed = sem("consts_landed")
        out_landed = sem("out_landed")
        pool_consts = sem("pool_consts")
        act_consts = sem("act_consts")
        dve_consts = sem("dve_consts")
        hi_ready = sem("hi_ready")
        lo_ready = sem("lo_ready")
        unit_used = sem("unit_used")
        s_hi_ready = sem("s_hi_ready")
        s_lo_ready = sem("s_lo_ready")
        acc_free = sem("acc_free")
        row_step = sem("row_step")
        rows_summed = sem("rows_summed")
        deg_ready = sem("deg_ready")
        deg1_ready = sem("deg1_ready")
        d_ready = sem("d_ready")
        o_turned = sem("o_turned")
        relu_ready = sem("relu_ready")
        post_step = [sem(f"post_step{n}") for n in range(LAYERS)]
        post_tanh = sem("post_tanh")
        x_ready = sem("x_ready")
        stats_ready = sem("stats_ready")
        mv_ready = sem("mv_ready")
        var_ready = sem("var_ready")
        rstd_ready = sem("rstd_ready")
        scale_ready = sem("scale_ready")
        ln_ready = sem("ln_ready")
        h_ready = sem("h_ready")
        h_turned = sem("h_turned")
        hT_ready = sem("hT_ready")
        m_ready = sem("m_ready")
        hyp_sq = sem("hyp_sq")
        hyp_step = sem("hyp_step")
        hyp_to_pool = sem("hyp_to_pool")
        hyp_pow = sem("hyp_pow")
        hyp_to_act = sem("hyp_to_act")
        hyp_act = sem("hyp_act")
        s_next_ready = sem("s_next_ready")
        bias_step = sem("bias_step")
        bias_pow = sem("bias_pow")
        bias_tanh = sem("bias_tanh")

        HYP_TO_ACT = 3 * SLABS
        LINKS = {0: 1, 1: 8, 2: 1, 3: 0}

        def rows(t, slab, k=None):
            return t[:, bass.ds(slab * TILES, TILES), :] if k is None else t[:, bass.ds(slab * TILES + k, 1), :]

        def d_of(slab, k=None):
            return scale_d[:, bass.ds(slab * TILES, TILES)] if k is None else scale_d[:, bass.ds(slab * TILES + k, 1)]

        def source0(unit):
            i, c, hh = unit
            if c == LAST:
                return res[:, i, hh * UNIT:(hh + 1) * UNIT], res_landed, 16 * (i + 1)
            if c == i:
                return diag[:, hh * UNIT:(hh + 1) * UNIT], diag_landed, 16 * (i + 1)
            n = RING0.index(unit) if c < i else len(RING0) - 1 - RING0[::-1].index(unit)
            return raw[:, n % RING, :], raw_landed[n % RING], 16 * (n // RING + 1)

        def source(layer, slab, u, chunks):
            c, hh = chunks[u // 2], u % 2
            if c == LAST:
                return res[:, bass.ds(slab, 1), hh * UNIT:(hh + 1) * UNIT], None, None
            r = u - (2 if LAST in chunks[:u // 2] else 0)
            return raw[:, r % RING:r % RING + 1, :], raw_landed[r % RING], (ring_laps(layer, slab) + r // RING + 1) * 16

        def slabs_of(eng, layer, body):
            body(layer, 0, slab0_chunks(layer))
            with eng.Fori(0, (SLABS - 2) // 2) as it:
                body(layer, it * 2 + 1, list(range(CHUNKS)), 1)
                body(layer, it * 2 + 2, list(range(CHUNKS)), 0)
            body(layer, SLABS - 1, list(range(CHUNKS)))

        WINDOW = 7
        AT = dict(turn_o=1, relu=4, tanh=5, x=4, ln=5, h=7, turn_h=5, hT=8, times_w=7, s_next=11,
                  hyp1=9, hyp2=10, hyp3=11, hyp4=12, hyp5=12, hyp6=13)
        AT0 = dict(turn_o=0, x=3, ln=4, h=4, turn_h=3, hT=5, times_w=5, s_next=6,
                   hyp1=6, hyp2=7, hyp3=8, hyp4=9, hyp5=10, hyp6=11)

        def second_pass(do_unit, after):
            for u in range(len(SPLIT0) - PASS1_SPLIT):
                do_unit(PASS1_SPLIT + u)
                for n in range(SLABS - 1):
                    after(n, LAST - n, u - WINDOW * n, AT0)

        block = ctx.enter_context(nc.Block())

        @block.sync
        def _(sp):
            def load_unit(slot, row, user, used, landed):
                if user is not None:
                    sp.wait_ge(user, used)
                sp.dma_start(raw[:, slot, :], adj[bass.ds(row, P), :]).then_inc(landed, 16)

            def row_of(i, c, hh):
                return ((i * CHUNKS + c) * 2 + hh) * P

            def user_of(n):
                i, c, _ = RING0[n]
                if n < PASS1_RING and c > i:
                    return row_step, ROW_STEPS[RING0[n]]
                return lo_ready, SPLIT0.index(RING0[n]) + 1

            def load0(n):
                user, used = user_of(n - RING) if n >= RING else (None, None)
                load_unit(n % RING, row_of(*RING0[n]), user, used, raw_landed[n % RING])

            sp.dma_start(x[:], x_in).then_inc(consts_landed, 16)
            sp.dma_start(w[:], w_in).then_inc(consts_landed, 16)
            sp.dma_start(bias[:], bias_in).then_inc(consts_landed, 16)
            n = 0
            for i in range(SLABS):
                while n < PASS1_RING and RING0[n][0] == i:
                    load0(n)
                    n += 1
                both = adj[row_of(i, LAST, 0):row_of(i, LAST, 0) + 2 * P, :].rearrange("(h p) n -> p h n", p=P)
                if i < LAST:
                    if i >= 1:
                        sp.wait_ge(lo_ready, SPLIT0.index((i - 1, i - 1, 1)) + 1)
                    sp.dma_start(res[:, i, :].rearrange("p (h n) -> p h n", h=2), both).then_inc(res_landed, 16)
                    both = adj[row_of(i, i, 0):row_of(i, i, 0) + 2 * P, :].rearrange("(h p) n -> p h n", p=P)
                    sp.dma_start(diag[:].rearrange("p (h n) -> p h n", h=2), both).then_inc(diag_landed, 16)
                else:
                    sp.dma_start(res[:, i, :].rearrange("p (h n) -> p h n", h=2), both).then_inc(res_landed, 16)
            for n in range(PASS1_RING, len(RING0)):
                load0(n)

            def body(layer, slab, chunks, parity=None):
                skip = 2 if layer == 1 else 0
                first = isinstance(slab, int) and slab == 0
                for r, (c, hh) in enumerate((c, hh) for c in chunks if c != LAST for hh in range(2)):
                    if r >= RING:
                        u = r - RING + (skip if first else 0)
                        user, used = lo_ready, split_index(layer, slab, u) + 1
                    elif first and layer == 1:
                        user, used = user_of(len(RING0) - RING + r)
                    else:
                        user, used = lo_ready, split_index(layer, slab, r + RING + skip) - UNITS_PER_SLAB + 1
                    load_unit(r % RING, slab * (CHUNKS * 2 * P) + (c * 2 + hh) * P, user, used, raw_landed[r % RING])

            for layer in range(1, LAYERS):
                slabs_of(sp, layer, body)

        @block.scalar
        def _(act):
            def split_hi(src, landed, value, g, slot):
                if landed is not None:
                    act.wait_ge(landed, value)
                if not isinstance(g, int) or g >= SPLIT:
                    act.wait_ge(unit_used, g - SPLIT + 1)
                nc.scalar.copy(hi[:, slot:slot + 1, :] if len(src.shape) == 3 else hi[:, slot, :], src).then_inc(hi_ready, 1)

            def free_acc(units, bank, dst):
                act.wait_ge(unit_used, units)
                nc.scalar.copy(dst, acc[bank][:]).then_inc(acc_free, 1)

            def squares(src, at):
                for k in range(TILES):
                    last = nc.scalar.activation(junk_a[:, at + k, :], src[:, k, :], ACT.Square, accum_out=sq[:, at + k:at + k + 1])
                return last

            def h_step(p, slab):
                act.wait_ge(ln_ready, p + 1)
                if not isinstance(p, int) or p >= 1:
                    act.wait_ge(h_turned, p)
                for k in range(TILES):
                    last = nc.scalar.activation(h[:, k:k + 1, :], rows(x, slab, k), ACT.Relu,
                                                bias=ln_bias[:, k:k + 1], scale=ln_scale[:, k:k + 1])
                last.then_inc(h_ready, 1)

            def hT_step(p):
                act.wait_ge(h_turned, p + 1)
                if not isinstance(p, int) or p >= 1:
                    act.wait_ge(m_ready, p)
                nc.scalar.copy(hT[:], h_ps[:]).then_inc(hT_ready, 1)

            def s_next_step(p, slab, seen):
                act.wait_ge(m_ready, p + 1)
                if seen is not None:
                    act.wait_ge(s_lo_ready, seen)
                nc.scalar.copy(rows(s_next, slab), m_ps[:]).then_inc(s_next_ready, 1)

            def split_s(layer, slab):
                m = layer * SLABS + place(layer, slab)
                act.wait_ge(s_next_ready, m + 1)
                nc.scalar.copy(rows(s_hi, slab), rows(s_next, slab)).then_inc(s_hi_ready, 1)

            def after(n, slab, at, table, layer=1):
                p = n + SLABS
                if layer == 2 and at == table["relu"]:
                    act.wait_ge(o_turned, n + 1)
                    act.wait_ge(h_turned, p)
                    act.wait_ge(hyp_pow, n + SLABS)
                    nc.scalar.activation(h[:], o_ps[:], ACT.Relu).then_inc(relu_ready, 1)
                    squares(o_ps, 0)
                    act.wait_ge(relu_ready, 2 * (n - SLABS) + 1)
                    squares(h, TILES).then_inc(relu_ready, 1)
                if layer == 2 and at == table["tanh"]:
                    act.wait_ge(hyp_to_act, HYP_TO_ACT + n - SLABS + 1)
                    nc.scalar.activation(hyp[:, 2, :], hyp[:, 1, :], ACT.Tanh).then_inc(post_tanh, 1)
                if at == table["h"]:
                    h_step(p, slab)
                    if layer == 1:
                        if n >= 1:
                            act.wait_ge(hyp_to_pool, 2 * n - 1)
                        act.wait_ge(h_ready, p + 1)
                        squares(h, 0).then_inc(hyp_sq, 1)
                if at == table["hT"]:
                    hT_step(p)
                if layer != 1 and at == table["s_next"]:
                    s_next_step(p, slab, layer * SLABS)
                if layer == 1:
                    if at == table["hyp1"]:
                        act.wait_ge(m_ready, p + 1)
                        squares(m_ps, TILES).then_inc(hyp_sq, 1)
                    if at == table["hyp2"]:
                        act.wait_ge(hyp_to_act, 3 * n + 1)
                        nc.scalar.activation(hyp[:, 1, :], hyp[:, 0, :], ACT.Ln, bias=1.0)
                        nc.scalar.activation(hyp[:, 2, :], hyp[:, 0, :], ACT.Ln, bias=1.0, scale=-1.0).then_inc(hyp_act, 1)
                    if at == table["hyp3"]:
                        act.wait_ge(hyp_to_act, 3 * n + 2)
                        nc.scalar.activation(hyp[:, 8, :], hyp[:, 7, :], ACT.Tanh).then_inc(hyp_act, 1)
                    if at == table["hyp5"]:
                        act.wait_ge(hyp_pow, 2 * n + 2)
                        nc.scalar.activation(hyp[:, 20, :], hyp[:, 18, :], ACT.Ln, bias=1.0)
                        nc.scalar.activation(hyp[:, 21, :], hyp[:, 16, :], ACT.Ln).then_inc(hyp_act, 1)
                    if at == table["hyp6"]:
                        act.wait_ge(hyp_to_act, 3 * n + 3)
                        for k in range(TILES):
                            last = nc.scalar.activation(rows(s_next, slab, k), m_ps[:, k:k + 1, :], ACT.Copy,
                                                        scale=hyp[:, 24, k:k + 1])
                        last.then_inc(hyp_act, 1)

            act.wait_ge(pool_consts, 2)
            nc.scalar.copy(ident_r[:], ident[:])
            nc.scalar.mul(mean_r[:], ones[:], 1.0 / P).then_inc(act_consts, 1)
            act.wait_ge(consts_landed, 48)
            nc.scalar.activation(junk_a[:, 0, :], bias[:, 1, :], ACT.Square, accum_out=bstat[:, 0:1]).then_inc(bias_step, 1)
            act.wait_ge(bias_step, 3)
            nc.scalar.activation(bstat[:, 4:5], bstat[:, 3:4], ACT.Tanh).then_inc(bias_tanh, 1)

            def prep0(i):
                h_step(i, i)
                hT_step(i)
                s_next_step(i, i, None)

            def split0(g):
                src, landed, value = source0(SPLIT0[g])
                split_hi(src, landed, value, g, g % SPLIT)

            prep0(0)
            g = 0
            for i in range(SLABS + 1):
                if i >= 1:
                    act.wait_ge(s_next_ready, i)
                    act.wait_ge(d_ready, i)
                    for k in range(TILES):
                        last = nc.scalar.activation(rows(s_hi, i - 1, k), rows(s_next, i - 1, k), ACT.Copy,
                                                    scale=d_of(i - 1, k))
                    last.then_inc(s_hi_ready, 1)
                    for _ in range(2):
                        split0(g)
                        g += 1
                    diag_units = g
                if i < SLABS - 1:
                    prep0(i + 1)
                if i < SLABS:
                    for _ in range(2 * i):
                        split0(g)
                        g += 1
                if i >= 1:
                    act.wait_ge(s_lo_ready, i)
                    free_acc(diag_units, (i - 1) % 2, rows(s_next, i - 1).rearrange("p t f -> p (t f)"))

            second_pass(split0, lambda n, slab, at, table: after(n, slab, at, table))

            def body(layer, slab, chunks, parity=None):
                if isinstance(slab, int):
                    parity = slab % 2
                n = (layer * SLABS + slab - 1)
                prev, lay = (slab - 1, layer + 1)
                if isinstance(slab, int) and slab == 0:
                    prev, lay = (0 if layer == 1 else LAST), layer
                for u in range(UNITS_PER_SLAB):
                    if isinstance(slab, int) and slab == 0 and u % 2 == 0:
                        split_s(layer, chunks[u // 2])
                    src, landed, value = source(layer, slab, u, chunks)
                    split_hi(src, landed, value, split_index(layer, slab, u), u % SPLIT)
                    if u == 3 and not (isinstance(slab, int) and slab == 0 and layer == 1):
                        act.wait_ge(o_turned, n)
                        free_acc(split_index(layer, slab, 0), parity, o_sb[:])
                    if lay < LAYERS:
                        after(n, prev, u, AT, lay)
                    elif u == AT["h"]:
                        send(n, prev)

            def send(n, slab):
                act.wait_ge(x_ready, n + 1)
                act.dma_start(out[:, bass.ds(slab * TILES, TILES), :], rows(x, slab)).then_inc(out_landed, 16)

            for layer in range(1, LAYERS):
                slabs_of(act, layer, body)
            n = LAYERS * SLABS - 1
            act.wait_ge(o_turned, n)
            free_acc(split_index(LAYERS, 0, 0), (evac_index(LAYERS, 0) - 1) % 2, o_sb[:])
            send(n, LAST)
            act.wait_ge(out_landed, 16 * SLABS)

        @block.vector
        def _(dve):
            steps = {}

            def link(s, ins, base=0):
                steps[s.name] = steps.get(s.name, 0) + 1
                ins.then_inc(s, 1)
                dve.wait_ge(s, base + steps[s.name])

            def split_lo(src, g, slot):
                dve.wait_ge(hi_ready, g + 1)
                flat = len(src.shape) == 2
                hs = hi[:, slot, :] if flat else hi[:, slot:slot + 1, :]
                ls = lo[:, slot, :] if flat else lo[:, slot:slot + 1, :]
                last = nc.vector.tensor_tensor(ls, src, hs.bitcast(FP32), ALU.subtract)
                last.then_inc(lo_ready, 1)
                return last

            def x_step(n, slab, layer):
                src = layer - 1
                base = (n - src * SLABS) * LINKS[src]
                steps[post_step[src].name] = 0
                dve.wait_ge(o_turned, n + 1)
                xs = rows(x, slab)
                if src in (0, 2):
                    dve.wait_ge(h_turned, n + SLABS)
                    if src == 0 and n >= 1:
                        dve.wait_ge(hyp_sq, 2 * n - 1)
                    for k in range(TILES):
                        last = nc.vector.scalar_tensor_tensor(h[:, k:k + 1, :], o_ps[:, k:k + 1, :], d_of(slab, k),
                                                              bias[:, src:src + 1, :], ALU.mult, ALU.add)
                    link(post_step[src], last, base)
                    if src == 0:
                        last = nc.vector.scalar_tensor_tensor(xs, h[:], 0.0, xs, ALU.max, ALU.add)
                    else:
                        last = nc.vector.tensor_tensor(xs, h[:], xs, ALU.add)
                if src == 3:
                    last = nc.vector.scalar_tensor_tensor(xs, o_ps[:], 0.0, xs, ALU.max, ALU.add)
                if src == 1:
                    q = n - SLABS
                    st = post_step[1]
                    dve.wait_ge(relu_ready, 2 * q + 2)
                    last = nc.vector.tensor_scalar(sq[:], sq[:], TINY2, None, ALU.max)
                    last.then_inc(hyp_to_pool, 1)
                    dve.wait_ge(hyp_pow, 2 * SLABS + q + 1)
                    link(st, nc.vector.reciprocal(hyp[:, 4, :], nrm[:, 0:TILES]), base)
                    link(st, nc.vector.tensor_scalar(hyp[:, 5, :], nrm[:, 0:TILES], ATANH_MAX, None, ALU.min), base)
                    link(st, nc.vector.tensor_tensor(hyp[:, 6, :], hyp[:, 5, :], hyp[:, 4, :], ALU.mult), base)
                    link(st, nc.vector.tensor_tensor(hyp[:, 7, :], hyp[:, 6, :], nrm[:, TILES:2 * TILES], ALU.mult), base)
                    nc.vector.tensor_scalar(hyp[:, 1, :], hyp[:, 7, :], TINY, None, ALU.max).then_inc(hyp_to_act, 1)
                    dve.wait_ge(post_tanh, q + 1)
                    link(st, nc.vector.reciprocal(hyp[:, 8, :], hyp[:, 1, :]), base)
                    link(st, nc.vector.tensor_scalar(hyp[:, 9, :], hyp[:, 2, :], MAXNORM, None, ALU.min), base)
                    link(st, nc.vector.tensor_tensor(hyp[:, 10, :], hyp[:, 9, :], hyp[:, 8, :], ALU.mult), base)
                    link(st, nc.vector.tensor_tensor(hyp[:, 11, :], hyp[:, 10, :], hyp[:, 6, :], ALU.mult), base)
                    for k in range(TILES):
                        xk = rows(x, slab, k)
                        last = nc.vector.scalar_tensor_tensor(xk, h[:, k:k + 1, :], hyp[:, 11, k:k + 1], xk,
                                                              ALU.mult, ALU.add)
                last.then_inc(x_ready, 1)
                assert steps[post_step[src].name] == LINKS[src], steps

            def carry_wait():
                nc.vector.memset(spare[:], 0.0)

            def stats_step(p, slab, xr):
                if xr is not None:
                    dve.wait_ge(x_ready, xr)
                    carry_wait()
                for k in range(TILES):
                    last = nc.vector.bn_stats(stats[:, k, :], rows(x, slab, k))
                last.then_inc(stats_ready, 1)
                dve.wait_ge(stats_ready, p + 1)
                carry_wait()
                for k in range(TILES):
                    last = nc.vector.bn_aggr(mv[:, k, :], stats[:, k, :])
                last.then_inc(mv_ready, 1)
                dve.wait_ge(mv_ready, p + 1)
                nc.vector.tensor_scalar(var_eps[:], mv[:, :, 1], LN_EPS, None, ALU.add).then_inc(var_ready, 1)

            def ln_step(p, slab, layer):
                dve.wait_ge(rstd_ready, p + 1)
                if not isinstance(p, int) or p >= 1:
                    dve.wait_ge(h_ready, p)
                if layer == 2:
                    nc.vector.tensor_tensor(ln_scale[:], rstd[:], d_of(slab), ALU.mult).then_inc(scale_ready, 1)
                else:
                    nc.vector.tensor_copy(ln_scale[:], rstd[:]).then_inc(scale_ready, 1)
                dve.wait_ge(scale_ready, p + 1)
                nc.vector.scalar_tensor_tensor(ln_bias[:], mv[:, :, 0], -1.0, ln_scale[:], ALU.mult,
                                               ALU.mult).then_inc(ln_ready, 1)

            def V(i):
                return hyp[:, i, :]

            def tt(o, a, b, op):
                link(hyp_step, nc.vector.tensor_tensor(o, a, b, op))

            def ts(o, a, s1, s2, op0, op1=None):
                if op1 is None:
                    link(hyp_step, nc.vector.tensor_scalar(o, a, s1, s2, op0))
                else:
                    link(hyp_step, nc.vector.tensor_scalar(o, a, s1, s2, op0, op1))

            def stt(o, a, s, b, op0, op1):
                link(hyp_step, nc.vector.scalar_tensor_tensor(o, a, s, b, op0, op1))

            def series(o, u, t):
                ts(t, u, SERIES[0], None, ALU.mult)
                for coef in SERIES[1:-1]:
                    stt(t, t, coef, u, ALU.add, ALU.mult)
                ts(o, t, 1.0, None, ALU.add)

            def choose(o, v, small, big, t, t2):
                ts(t, v, SERIES_BELOW, None, ALU.is_lt)
                tt(t2, small, big, ALU.subtract)
                tt(t2, t2, t, ALU.mult)
                tt(o, t2, big, ALU.add)

            def hyp1(n):
                dve.wait_ge(hyp_sq, 2 * n + 2)
                for k in range(TILES):
                    last = nc.vector.scalar_tensor_tensor(junk_v[:, k, :], m_ps[:, k, :], 1.0, hyp_b[:, 0, :], ALU.mult,
                                                          ALU.mult, accum_out=hyp[:, 3, k:k + 1])
                link(hyp_step, last)
                nc.vector.tensor_scalar(hyp[:, 4:6, :].rearrange("p a b -> p (a b)"), sq[:], TINY2, None,
                                        ALU.max).then_inc(hyp_to_pool, 1)

            def hyp2(n):
                dve.wait_ge(hyp_pow, 2 * n + 1)
                nc.vector.tensor_scalar(V(0), nrm[:, 0:TILES], CLIP, None, ALU.min).then_inc(hyp_to_act, 1)
                link(hyp_step, nc.vector.reciprocal(hyp[:, 9:11, :].rearrange("p a b -> p (a b)"), nrm[:]))
                series(V(11), V(4), V(12))

            def hyp3(n):
                dve.wait_ge(hyp_act, 4 * n + 1)
                tt(V(13), V(1), V(2), ALU.subtract)
                stt(V(13), V(13), 0.5, V(9), ALU.mult, ALU.mult)
                choose(V(13), nrm[:, 0:TILES], V(11), V(13), V(12), V(14))
                nc.vector.tensor_tensor(V(7), V(13), nrm[:, TILES:2 * TILES], ALU.mult).then_inc(hyp_to_act, 1)

            def hyp4(n):
                dve.wait_ge(hyp_act, 4 * n + 2)
                ts(V(12), V(8), MAXNORM, None, ALU.min)
                tt(V(11), V(12), V(10), ALU.mult)
                tt(V(12), V(11), V(11), ALU.mult)
                tt(V(12), V(12), V(5), ALU.mult)
                tt(V(13), V(11), V(3), ALU.mult)
                ts(V(13), V(13), 2.0, 1.0, ALU.mult, ALU.add)
                ts(V(14), V(13), bstat[:, 8:9], None, ALU.add)
                ts(V(15), V(12), -1.0, 1.0, ALU.mult, ALU.add)
                stt(V(13), V(12), bstat[:, 8:9], V(13), ALU.mult, ALU.add)
                ts(V(13), V(13), TINY, None, ALU.max)
                link(hyp_step, nc.vector.reciprocal(V(13), V(13)))
                tt(V(14), V(14), V(11), ALU.mult)
                tt(V(14), V(14), V(13), ALU.mult)
                ts(V(16), V(15), bstat[:, 9:10], None, ALU.mult)
                tt(V(15), V(15), V(13), ALU.mult)
                tt(V(16), V(16), V(13), ALU.mult)
                tt(V(17), V(14), V(3), ALU.mult)
                ts(V(19), V(15), bstat[:, 8:9], None, ALU.mult)
                stt(V(17), V(17), 2.0, V(19), ALU.mult, ALU.add)
                tt(V(17), V(17), V(15), ALU.mult)
                tt(V(19), V(14), V(14), ALU.mult)
                tt(V(19), V(19), V(5), ALU.mult)
                tt(V(17), V(17), V(19), ALU.add)
                nc.vector.tensor_scalar(V(17), V(17), TINY2, None, ALU.max).then_inc(hyp_to_pool, 1)

            def hyp5(n):
                dve.wait_ge(hyp_to_pool, 2 * n + 2)
                series(V(11), V(17), V(12))
                dve.wait_ge(hyp_pow, 2 * n + 2)
                link(hyp_step, nc.vector.reciprocal(V(19), V(18)))
                dve.wait_ge(hyp_act, 4 * n + 3)
                stt(V(22), V(21), -0.5, V(20), ALU.mult, ALU.add)
                ts(V(22), V(22), ATANH_MAX, None, ALU.min)
                tt(V(22), V(22), V(19), ALU.mult)
                choose(V(22), V(18), V(11), V(22), V(12), V(13))
                tt(V(25), V(22), V(15), ALU.mult)
                nc.vector.tensor_tensor(V(24), V(22), V(14), ALU.mult).then_inc(hyp_to_act, 1)

            def hyp6(n, slab):
                dve.wait_ge(hyp_act, 4 * n + 4)
                for k in range(TILES):
                    sk = rows(s_next, slab, k)
                    last = nc.vector.scalar_tensor_tensor(sk, hyp_b[:], hyp[:, 25, k:k + 1], sk, ALU.mult, ALU.add)
                last.then_inc(s_next_ready, 1)

            def after(n, slab, at, table, layer=1):
                p = n + SLABS
                if at == table["x"]:
                    x_step(n, slab, layer)
                    if layer < LAYERS:
                        stats_step(p, slab, n + 1)
                if layer < LAYERS and at == table["ln"]:
                    ln_step(p, slab, layer)
                if layer == 1:
                    for k, step in enumerate((hyp1, hyp2, hyp3, hyp4, hyp5)):
                        if at == table[f"hyp{k + 1}"]:
                            step(n)
                    if at == table["hyp6"]:
                        hyp6(n, slab)

            def split_s(layer, slab):
                m = layer * SLABS + place(layer, slab)
                dve.wait_ge(s_hi_ready, m + 1)
                nc.vector.tensor_tensor(rows(s_lo, slab), rows(s_next, slab), rows(s_hi, slab).bitcast(FP32),
                                        ALU.subtract).then_inc(s_lo_ready, 1)

            nc.vector.memset(half[:], 0.5)
            nc.vector.memset(minus_half[:], -0.5).then_inc(dve_consts, 1)
            dve.wait_ge(bias_step, 1)
            nc.vector.tensor_scalar(bstat[:, 1:2], bstat[:, 0:1], TINY2, None, ALU.max).then_inc(bias_step, 1)
            dve.wait_ge(bias_pow, 1)
            nc.vector.tensor_scalar(bstat[:, 3:4], bstat[:, 2:3], 1.0, None, ALU.mult).then_inc(bias_step, 1)
            dve.wait_ge(bias_step, 3)
            nc.vector.reciprocal(bstat[:, 5:6], bstat[:, 3:4]).then_inc(bias_step, 1)
            dve.wait_ge(bias_tanh, 1)
            nc.vector.tensor_scalar(bstat[:, 6:7], bstat[:, 4:5], MAXNORM, None, ALU.min).then_inc(bias_step, 1)
            dve.wait_ge(bias_step, 5)
            nc.vector.tensor_tensor(bstat[:, 7:8], bstat[:, 6:7], bstat[:, 5:6], ALU.mult).then_inc(bias_step, 1)
            dve.wait_ge(bias_step, 6)
            nc.vector.tensor_scalar(hyp_b[:, 0, :], bias[:, 1, :], bstat[:, 7:8], None, ALU.mult).then_inc(bias_step, 1)
            dve.wait_ge(bias_step, 7)
            nc.vector.scalar_tensor_tensor(junk_v[:, 0, :], hyp_b[:, 0, :], 1.0, hyp_b[:, 0, :], ALU.mult, ALU.mult,
                                           accum_out=bstat[:, 8:9]).then_inc(bias_step, 1)
            dve.wait_ge(bias_step, 8)
            nc.vector.tensor_scalar(bstat[:, 9:10], bstat[:, 8:9], -1.0, 1.0, ALU.mult, ALU.add).then_inc(bias_step, 1)
            dve.wait_ge(bias_step, 9)

            dve.wait_ge(consts_landed, 48)
            stats_step(0, 0, None)
            ln_step(0, 0, 0)
            ring_n, g = 0, 0
            fresh = [True]

            def add_rows(src, landed, value, final=False):
                dve.wait_ge(landed, value)
                a, b = src[:, 0:SLAB], src[:, SLAB:UNIT]
                if fresh[0]:
                    link(row_step, nc.vector.tensor_tensor(row_part[:], a, b, ALU.add))
                else:
                    link(row_step, nc.vector.tensor_tensor(row_part[:], row_part[:], a, ALU.add))
                    last = nc.vector.tensor_tensor(row_part[:], row_part[:], b, ALU.add)
                    if final:
                        last.then_inc(rows_summed, 1)
                    else:
                        link(row_step, last)
                fresh[0] = False

            for i in range(SLABS + 1):
                fresh[0] = True
                if i < SLABS:
                    for c in range(i + 1, LAST):
                        for hh in range(2):
                            src, landed, value = raw[:, ring_n % RING, :], raw_landed[ring_n % RING], 16 * (ring_n // RING + 1)
                            add_rows(src, landed, value)
                            ring_n += 1
                if i < SLABS - 1:
                    stats_step(i + 1, i + 1, None)
                if i >= 1:
                    dve.wait_ge(s_hi_ready, i)
                    for k in range(TILES):
                        last = nc.vector.scalar_tensor_tensor(rows(s_lo, i - 1, k), rows(s_next, i - 1, k), d_of(i - 1, k),
                                                              rows(s_hi, i - 1, k).bitcast(FP32), ALU.mult, ALU.subtract)
                    last.then_inc(s_lo_ready, 1)
                    for hh in range(2):
                        src, _, _ = source0(SPLIT0[g])
                        split_lo(src, g, g % SPLIT)
                        g += 1
                if i < SLABS - 1:
                    ln_step(i + 1, i + 1, 0)
                if i < SLABS:
                    for _ in range(2 * min(i, LAST)):
                        src, _, _ = source0(SPLIT0[g])
                        split_lo(src, g, g % SPLIT)
                        g += 1
                        ring_n += 1
                    for hh in range(2):
                        add_rows(res[:, i, hh * UNIT:(hh + 1) * UNIT], res_landed, 16 * (i + 1))
                    if i < LAST:
                        for hh in range(2):
                            add_rows(diag[:, hh * UNIT:(hh + 1) * UNIT], diag_landed, 16 * (i + 1),
                                     final=i == 0 and hh == 1)
                    if i >= 1:
                        dve.wait_ge(unit_used, g)
                        nc.vector.tensor_tensor(row_part[:], row_part[:], row_ps[:], ALU.add).then_inc(rows_summed, 1)
                    dve.wait_ge(deg_ready, i + 1)
                    nc.vector.tensor_scalar(deg1[:], deg_ps[:], 1.0, None, ALU.add).then_inc(deg1_ready, 1)

            def second_unit(gg):
                src, _, _ = source0(SPLIT0[gg])
                split_lo(src, gg, gg % SPLIT)
                for e in range(SLABS, EVACS0 - 1):
                    slab = SLABS - 2 - (e - SLABS)
                    end = PASS1_SPLIT + (LAST - slab) * (SLABS - slab)
                    if gg == end + SPLIT - 2:
                        join(e, slab, end)

            def join(e, slab, units):
                dve.wait_ge(unit_used, units)
                part = rows(s_next, slab).rearrange("p t f -> p (t f)")
                nc.vector.tensor_tensor(part, part, acc[e % 2][:], ALU.add).then_inc(acc_free, 1)

            dve.wait_ge(acc_free, SLABS)
            second_pass(second_unit, lambda n, slab, at, table: after(n, slab, at, table))

            def body(layer, slab, chunks, parity=None):
                n = layer * SLABS + slab - 1
                prev, lay = slab - 1, layer + 1
                first = isinstance(slab, int) and slab == 0
                if first:
                    prev, lay = (0 if layer == 1 else LAST), layer
                for u in range(UNITS_PER_SLAB):
                    if first and u % 2 == 0:
                        split_s(layer, chunks[u // 2])
                    src, _, value = source(layer, slab, u, chunks)
                    split_lo(src, split_index(layer, slab, u), u % SPLIT)
                    if first and layer == 1 and u == 2:
                        join(EVACS0 - 1, 0, len(SPLIT0))
                    after(n, prev, u, AT, lay)

            for layer in range(1, LAYERS):
                slabs_of(dve, layer, body)
            after(LAYERS * SLABS - 1, LAST, AT["x"], AT, LAYERS)

        @block.tensor
        def _(pe):
            def contract(bank, c, hh, slot, first, last_unit, g, rowsum=None):
                pe.wait_ge(lo_ready, g + 1)
                for t in range(2):
                    j = c * TILES + hh * 2 + t
                    a, b = hi[:, slot, t * SLAB:(t + 1) * SLAB], lo[:, slot, t * SLAB:(t + 1) * SLAB]
                    nc.tensor.matmul(acc[bank][:], s_hi[:, j, :], a, start=first and t == 0, stop=False)
                    nc.tensor.matmul(acc[bank][:], s_hi[:, j, :], b, start=False, stop=False)
                    last = nc.tensor.matmul(acc[bank][:], s_lo[:, j, :], a, start=False, stop=last_unit and t == 1)
                if rowsum is not None:
                    for t in range(2):
                        for k, part in enumerate((hi, lo)):
                            last = nc.tensor.matmul(row_ps[:], mean_r[:], part[:, slot, t * SLAB:(t + 1) * SLAB],
                                                    start=rowsum == 0 and t + k == 0, stop=rowsum == 2 and t + k == 2)
                last.then_inc(unit_used, 1)
                return last

            def turn_o(n, slab, own, src):
                pe.wait_ge(x_ready, n) if not isinstance(n, int) or n >= 1 else None
                for k in range(TILES):
                    last = nc.tensor.matmul(o_ps[:, k, :], src(k), ident[:], is_transpose=True, start=k == 0,
                                            stop=(not own) and k == TILES - 1)
                if own:
                    flat = o_ps[:].rearrange("p t f -> p (t f)")
                    nc.tensor.matmul(flat, ident_r[:], rows(s_hi, slab).rearrange("p t f -> p (t f)"), start=False, stop=False)
                    last = nc.tensor.matmul(flat, ident_r[:], rows(s_lo, slab).rearrange("p t f -> p (t f)"), start=False, stop=True)
                last.then_inc(o_turned, 1)

            def turn_h(p):
                pe.wait_ge(h_ready, p + 1)
                if not isinstance(p, int) or p >= 1:
                    pe.wait_ge(hT_ready, p)
                for k in range(TILES):
                    last = nc.tensor.matmul(h_ps[:, k * P:(k + 1) * P], h[:, k, :], ident[:], is_transpose=True,
                                            start=k == 0, stop=k == TILES - 1)
                last.then_inc(h_turned, 1)

            def times_w(p, layer):
                pe.wait_ge(hT_ready, p + 1)
                if not isinstance(p, int) or p >= 1:
                    pe.wait_ge(s_next_ready, p)
                for k in range(TILES):
                    last = nc.tensor.matmul(m_ps[:, k, :], hT[:, k * P:(k + 1) * P], w[:, layer, :],
                                            start=k == 0, stop=k == TILES - 1)
                last.then_inc(m_ready, 1)

            def after(n, slab, at, table, layer=1):
                if at == table["turn_o"]:
                    if layer == 1:
                        pe.wait_ge(acc_free, SLABS + n)
                        turn_o(n, slab, True, lambda k: s_next[:, slab * TILES + k, :])
                    else:
                        pe.wait_ge(acc_free, EVACS0 - SLABS + n + 1)
                        turn_o(n, slab, layer == 3, lambda k: o_sb[:, k * P:(k + 1) * P])
                if layer < LAYERS and at == table["turn_h"]:
                    turn_h(n + SLABS)
                if layer < LAYERS and at == table["times_w"]:
                    times_w(n + SLABS, layer)

            pe.wait_ge(pool_consts, 2)
            pe.wait_ge(consts_landed, 48)
            turn_h(0)
            times_w(0, 0)
            pe.wait_ge(act_consts, 1)
            g = 0
            for i in range(SLABS + 1):
                if i >= 1:
                    pe.wait_ge(s_lo_ready, i)
                    for hh in range(2):
                        last = contract((i - 1) % 2, i - 1, hh, g % SPLIT, i == 1 and hh == 0, hh == 1, g)
                        g += 1
                if i < SLABS - 1:
                    turn_h(i + 1)
                    times_w(i + 1, 0)
                if 1 <= i < SLABS:
                    if i >= 2:
                        pe.wait_ge(acc_free, i - 1)
                    pe.wait_ge(rows_summed, i)
                    for u in range(2 * i):
                        last = contract(i % 2, u // 2, u % 2, g % SPLIT, u == 0, False, g,
                                        rowsum=0 if u == 0 else 2 if u == 2 * i - 1 else 1)
                        g += 1
                if i < SLABS:
                    pe.wait_ge(rows_summed, i + 1)
                    if i >= 1:
                        pe.wait_ge(deg1_ready, i)
                    for k in range(TILES):
                        last = nc.tensor.matmul(deg_ps[:, k:k + 1], row_part[:, k * P:(k + 1) * P], ones[:, 0:1],
                                                start=k == 0, stop=k == TILES - 1)
                    last.then_inc(deg_ready, 1)

            def second_unit(gg):
                i, c, hh = SPLIT0[gg]
                e = SLABS + (SLABS - 2 - i)
                if c == LAST and hh == 0:
                    pe.wait_ge(acc_free, e - 1)
                end = c == i + 1 and hh == 1
                contract(e % 2, c, hh, gg % SPLIT, c == LAST and hh == 0, end, gg)

            second_pass(second_unit, lambda n, slab, at, table: after(n, slab, at, table))

            def body(layer, slab, chunks, parity=None):
                if isinstance(slab, int):
                    parity = slab % 2
                bank = 1 - parity
                first = isinstance(slab, int) and slab == 0
                n = layer * SLABS + slab - 1
                prev, lay = slab - 1, layer + 1
                if first:
                    prev, lay = (0 if layer == 1 else LAST), layer
                pe.wait_ge(acc_free, evac_index(layer, slab) - 1)
                for u in range(UNITS_PER_SLAB):
                    c = chunks[u // 2]
                    if first and u % 2 == 0:
                        pe.wait_ge(s_lo_ready, layer * SLABS + u // 2 + 1)
                    contract(bank, c, u % 2, u % SPLIT, u == 0, u == UNITS_PER_SLAB - 1, split_index(layer, slab, u))
                    after(n, prev, u, AT, lay)

            for layer in range(1, LAYERS):
                slabs_of(pe, layer, body)
            after(LAYERS * SLABS - 1, LAST, AT["turn_o"], AT, LAYERS)

        @block.gpsimd
        def _(pool):
            nc.gpsimd.memset(ones[:], 1.0).then_inc(pool_consts, 1)
            pool.wait_ge(pool_consts, 1)
            nc.gpsimd.affine_select(out=ident[:], in_=ones[:], compare_op=ALU.is_equal, fill=0.0, base=0,
                                    pattern=[[-1, P]], channel_multiplier=1).then_inc(pool_consts, 1)
            pool.wait_ge(dve_consts, 1)
            pool.wait_ge(bias_step, 2)
            nc.gpsimd.tensor_tensor(bstat[:, 2:3], bstat[:, 1:2], half[:, 0:1], ALU.pow).then_inc(bias_pow, 1)

            def rstd_step(p):
                pool.wait_ge(var_ready, p + 1)
                nc.gpsimd.tensor_tensor(rstd[:], var_eps[:], minus_half[:, 0:TILES], ALU.pow).then_inc(rstd_ready, 1)

            rstd_step(0)
            for i in range(SLABS):
                if i < SLABS - 1:
                    rstd_step(i + 1)
                pool.wait_ge(deg1_ready, i + 1)
                nc.gpsimd.tensor_tensor(d_of(i), deg1[:], minus_half[:, 0:TILES], ALU.pow).then_inc(d_ready, 1)
            order = []
            for n in range(SLABS):
                w0 = WINDOW * n
                t = AT0 if n < SLABS - 1 else {k: v + 0 for k, v in AT.items()}
                b = w0 if n < SLABS - 1 else 56
                order += [(b + t["x"], 0, n), (b + t["hyp1"], 1, n), (b + t["hyp4"], 2, n)]
            for _, kind, n in sorted(order):
                if kind == 0:
                    rstd_step(n + SLABS)
                elif kind == 1:
                    pool.wait_ge(hyp_to_pool, 2 * n + 1)
                    nc.gpsimd.tensor_tensor(nrm[:], hyp[:, 4:6, :].rearrange("p a b -> p (a b)"), half[:],
                                            ALU.pow).then_inc(hyp_pow, 1)
                else:
                    pool.wait_ge(hyp_to_pool, 2 * n + 2)
                    nc.gpsimd.tensor_tensor(hyp[:, 18, :], hyp[:, 17, :], half[:, 0:TILES], ALU.pow).then_inc(hyp_pow, 1)
            with pool.Fori(0, SLABS) as it:
                pool.wait_ge(hyp_to_pool, it + 2 * SLABS + 1)
                nc.gpsimd.tensor_tensor(nrm[:], sq[:], half[:], ALU.pow).then_inc(hyp_pow, 1)
                rstd_step(it + 2 * SLABS)
            with pool.Fori(0, SLABS) as it:
                rstd_step(it + 3 * SLABS)


def kernel(x, adj, L0_gnn_W, L0_gnn_b, L1_gnn_weight, L1_gnn_bias, L2_gnn_W, L2_gnn_b, L3_gnn_weights):
    import numpy as np
    import concourse.bacc as bacc
    from concourse.bass_utils import run_bass_kernel_spmd

    a = np.asarray(adj).reshape(SLABS, SLAB, CHUNKS, 2, 2, P).transpose(0, 2, 3, 5, 4, 1)
    arrays = {
        "adj_units": np.ascontiguousarray(a).reshape(SLABS * CHUNKS * 2 * P, UNIT),
        "x_rows": np.ascontiguousarray(np.asarray(x).reshape(N // P, P, F).transpose(1, 0, 2)),
        "weights": np.ascontiguousarray(np.stack([np.asarray(L0_gnn_W), np.asarray(L1_gnn_weight).T,
                                                  np.asarray(L2_gnn_W).T, np.asarray(L3_gnn_weights)], axis=1)),
        "biases": np.ascontiguousarray(np.broadcast_to(
            np.stack([np.asarray(L0_gnn_b), np.asarray(L1_gnn_bias), np.asarray(L2_gnn_b)]), (P, 3, F))),
    }
    nc = bacc.Bacc("TRN2", target_bir_lowering=False, num_devices=1,
                   dynamic_dma_scratch_size=4096)
    aps = [nc.dram_tensor(k, v.shape, FP32, kind="ExternalInput").ap() for k, v in arrays.items()]
    out = nc.dram_tensor("out_rows", (P, N // P, F), FP32, kind="ExternalOutput").ap()
    build(nc, *aps, out)
    r = run_bass_kernel_spmd(nc, [arrays], core_ids=[0])
    got = r.results[0]["out_rows"]
    return np.ascontiguousarray(got.transpose(1, 0, 2)).reshape(N, F)
```

```python
import concourse.bass as bass
from concourse import mybir
from contextlib import ExitStack

FP32 = mybir.dt.float32
FP32R = mybir.dt.float32r
ALU = mybir.AluOpType
ACT = mybir.ActivationFunctionType

N = 4096
F = 128
P = 128
LAYERS = 4
SLAB = 512
SLABS = N // SLAB
TILES = SLAB // P
CHUNKS = N // SLAB
UNIT = 2 * SLAB
LAST = CHUNKS - 1
RING = 7
SPLIT = 4
RING_PER_SLAB = 2 * LAST
UNITS_PER_SLAB = 2 * CHUNKS

LN_EPS = 1e-5
TINY = 1e-15
TINY2 = TINY * TINY
MAXNORM = 1.0 - 1e-5
CLIP = 1.0 - 1e-7
ATANH_MAX = 6.1030338227611125
SERIES_BELOW = 0.25
SERIES = [1.0 / 11, 1.0 / 9, 1.0 / 7, 1.0 / 5, 1.0 / 3]


def ring_order():
    units = []
    for i in range(SLABS):
        cs = list(range(i)) + list(range(i + 1, LAST))
        units += [(i, c, h) for c in cs for h in range(2)]
    for i in range(SLABS - 3, -1, -1):
        units += [(i, c, h) for c in range(LAST - 1, i, -1) for h in range(2)]
    return units


def split_order():
    units = []
    for i in range(SLABS + 1):
        below = [(i, c, h) for c in range(i) for h in range(2)] if i < SLABS else []
        units += below[:-2]
        if i:
            units += [(i - 1, i - 1, h) for h in range(2)]
        units += below[-2:]
    for i in range(SLABS - 2, -1, -1):
        units += [(i, c, h) for c in range(LAST, i, -1) for h in range(2)]
    return units


RING0 = ring_order()
SPLIT0 = split_order()
PASS1_RING = 2 * (6 * (SLABS - 1) + LAST)
PASS1_SPLIT = 2 * (SLABS * (SLABS - 1) // 2 + SLABS)
EVACS0 = 2 * SLABS - 1


ABOVE = [u for u in RING0[:PASS1_RING] if u[1] > u[0]]

AT = dict(turn_o=1, x=4, ln=6, h=8, turn_h=7, hT=10, times_w=9, s_next=12)
AT_HYP = dict(turn_o=1, relu=4, post1=5, post2=7, tanh=8, x=9, ln=11, h=12, turn_h=11, hT=14, times_w=13, s_next=15)
AT_HYP0 = dict(turn_o=1, relu=4, post1=4, post2=5, tanh=6, x=6, ln=7, h=8, turn_h=7, hT=9, times_w=9, s_next=11)

GROUPS = [(6, 2), (4, 2), (2, 2), (1, 1), (0, 1)]
PASS2 = len(SPLIT0) - PASS1_SPLIT
POST0 = dict(turn_o=0, x=3, ln=5, h=6, turn_h=5, hT=7, times_w=6, s_next=8)
POST0_LAST = dict(turn_o=1, x=4, ln=5, h=6, turn_h=5, hT=7, times_w=6, s_next=8)
HYP_PAIR = [9, 12, 14, 15, 17, 19]
HYP_ONE = [13, 15, 16, 17, 18, 19]
HYP_LAST = [8, 9, 10, 11, 12, 13]


def schedule():
    at = {}
    for n in range(SLABS):
        base, steps = (7 * n, POST0) if n < SLABS - 1 else (PASS2, POST0_LAST)
        for name, off in steps.items():
            at.setdefault(base + off, []).append((name, n))
    for q, (slab, width) in enumerate(GROUPS):
        n = LAST - slab
        base, offs = (7 * n, HYP_PAIR if width == 2 else HYP_ONE) if slab else (PASS2, HYP_LAST)
        for k, off in enumerate(offs):
            at.setdefault(base + off, []).append((f"hyp{k + 1}", q))
    return at


SCHEDULE = schedule()


def split_index(layer, slab, u):
    return layer * SLABS * UNITS_PER_SLAB + slab * UNITS_PER_SLAB + u


def ring_laps(layer, slab):
    return len(RING0) // RING + (layer - 1) * SLABS * RING_PER_SLAB // RING + slab * (RING_PER_SLAB // RING)


def evac_index(layer, slab):
    return EVACS0 + (layer - 1) * SLABS + slab


def slab0_chunks(layer):
    return list(range(LAST, -1, -1)) if layer == 1 else list(range(CHUNKS))


def place(layer, slab):
    return LAST - slab if layer == 1 else slab


def build(nc, adj, adj_rows, x_in, w_in, bias_in, out):
    ctx = ExitStack()
    with ctx:
        def sb(name, shape, dt=FP32):
            return ctx.enter_context(nc.sbuf_tensor(name, shape, dt))

        def pb(name, shape):
            return ctx.enter_context(nc.psum_tensor(name, shape, FP32))

        def sem(name):
            return ctx.enter_context(nc.semaphore(name))

        raw = sb("raw", [P, RING, UNIT])
        res = sb("res", [P, SLABS, 2 * UNIT])
        diag = sb("diag", [P, 2 * UNIT])
        hi = sb("hi", [P, SPLIT, UNIT], FP32R)
        lo = sb("lo", [P, SPLIT, UNIT], FP32R)
        x = sb("x", [P, N // P, F])
        s_next = sb("s_next", [P, N // P, F])
        s_hi = sb("s_hi", [P, N // P, F], FP32R)
        s_lo = sb("s_lo", [P, N // P, F], FP32R)
        w = sb("w", [P, LAYERS, F])
        bias = sb("bias", [P, 3, F])
        hyp_b = sb("hyp_b", [P, 1, F])
        o_sb = sb("o_sb", [P, SLAB])
        h = sb("h", [P, TILES, F])
        hT = sb("hT", [P, SLAB])
        above = sb("above", [P, 2, TILES, CHUNKS])
        above_sum = sb("above_sum", [P, TILES])
        row_part = o_sb
        ident = sb("ident", [P, P])
        ident_r = sb("ident_r", [P, P], FP32R)
        ones = sb("ones", [P, P])
        mean_r = sb("mean_r", [P, P], FP32R)
        scale_d = sb("scale_d", [P, N // P])
        deg1 = sb("deg1", [P, TILES])
        minus_half = sb("minus_half", [P, TILES])
        half = sb("half", [P, 2, 2 * TILES])
        stats = sb("stats", [P, TILES, 6])
        mv = sb("mv", [P, TILES, 2])
        var_eps = sb("var_eps", [P, TILES])
        rstd = sb("rstd", [P, TILES])
        ln_scale = sb("ln_scale", [P, TILES])
        ln_bias = sb("ln_bias", [P, TILES])
        spare = sb("spare", [P, 1])
        junk_a = sb("junk_a", [P, 2 * TILES, F])
        junk_v = sb("junk_v", [P, 2 * TILES, F])
        sq = sb("sq", [P, 2, 2 * TILES])
        nrm = sb("nrm", [P, 2, 2 * TILES])
        hyp = sb("hyp", [P, 32, 2 * TILES])
        bstat = sb("bstat", [P, 16])

        acc = [pb(f"acc{b}", [P, SLAB]) for b in range(2)]
        row_ps = pb("row_ps", [P, SLAB])
        deg_ps = pb("deg_ps", [P, TILES])
        o_ps = pb("o_ps", [P, TILES, P])
        h_ps = pb("h_ps", [P, SLAB])
        m_ps = pb("m_ps", [P, TILES, F])

        raw_landed = [sem(f"raw_landed{n}") for n in range(RING)]
        res_landed = sem("res_landed")
        diag_landed = sem("diag_landed")
        consts_landed = sem("consts_landed")
        out_landed = sem("out_landed")
        pool_consts = sem("pool_consts")
        act_consts = sem("act_consts")
        dve_consts = sem("dve_consts")
        hi_ready = sem("hi_ready")
        lo_ready = sem("lo_ready")
        unit_used = sem("unit_used")
        s_hi_ready = sem("s_hi_ready")
        s_lo_ready = sem("s_lo_ready")
        acc_free = sem("acc_free")
        row_step = sem("row_step")
        above_ready = sem("above_ready")
        above_summed = sem("above_summed")
        rows_summed = sem("rows_summed")
        deg_ready = sem("deg_ready")
        deg1_ready = sem("deg1_ready")
        d_ready = sem("d_ready")
        o_turned = sem("o_turned")
        relu_ready = sem("relu_ready")
        post_step = [sem(f"post_step{n}") for n in range(LAYERS)]
        post_tanh = sem("post_tanh")
        x_ready = sem("x_ready")
        stats_ready = sem("stats_ready")
        mv_ready = sem("mv_ready")
        var_ready = sem("var_ready")
        rstd_ready = sem("rstd_ready")
        scale_ready = sem("scale_ready")
        ln_ready = sem("ln_ready")
        h_ready = sem("h_ready")
        h_turned = sem("h_turned")
        hT_ready = sem("hT_ready")
        m_ready = sem("m_ready")
        hyp_sq = sem("hyp_sq")
        hyp_step = sem("hyp_step")
        hyp_to_pool = sem("hyp_to_pool")
        hyp_pow = sem("hyp_pow")
        hyp_to_act = sem("hyp_to_act")
        hyp_act = sem("hyp_act")
        m_copied = sem("m_copied")
        hyp_done = sem("hyp_done")
        bias_step = sem("bias_step")
        bias_pow = sem("bias_pow")
        bias_tanh = sem("bias_tanh")

        HYP_TO_ACT = 3 * len(GROUPS)
        HYP_TO_POOL = 2 * len(GROUPS)
        LINKS = {0: 1, 1: 6, 2: 1, 3: 0}

        def rows(t, slab, k=None):
            return t[:, bass.ds(slab * TILES, TILES), :] if k is None else t[:, bass.ds(slab * TILES + k, 1), :]

        def d_of(slab, k=None):
            return scale_d[:, bass.ds(slab * TILES, TILES)] if k is None else scale_d[:, bass.ds(slab * TILES + k, 1)]

        def source0(unit):
            i, c, hh = unit
            if c == LAST:
                return res[:, i, hh * UNIT:(hh + 1) * UNIT], res_landed, 16 * (i + 1)
            if c == i:
                return diag[:, hh * UNIT:(hh + 1) * UNIT], diag_landed, 16 * (i + 1)
            n = RING0.index(unit) if c < i else len(RING0) - 1 - RING0[::-1].index(unit)
            return raw[:, n % RING, :], raw_landed[n % RING], 16 * (n // RING + 1)

        def source(layer, slab, u, chunks):
            c, hh = chunks[u // 2], u % 2
            if c == LAST:
                return res[:, bass.ds(slab, 1), hh * UNIT:(hh + 1) * UNIT], None, None
            r = u - (2 if LAST in chunks[:u // 2] else 0)
            return raw[:, r % RING:r % RING + 1, :], raw_landed[r % RING], (ring_laps(layer, slab) + r // RING + 1) * 16

        def slabs_of(eng, layer, body):
            body(layer, 0, slab0_chunks(layer))
            with eng.Fori(0, (SLABS - 2) // 2) as it:
                body(layer, it * 2 + 1, list(range(CHUNKS)), 1)
                body(layer, it * 2 + 2, list(range(CHUNKS)), 0)
            body(layer, SLABS - 1, list(range(CHUNKS)))

        def table(layer, slab):
            first = isinstance(slab, int) and slab == 0
            if layer == (2 if first else 1):
                return AT_HYP0 if first else AT_HYP
            return AT

        block = ctx.enter_context(nc.Block())

        @block.sync
        def _(sp):
            def load_unit(slot, row, user, used, landed, adj=adj):
                if user is not None:
                    sp.wait_ge(user, used)
                sp.dma_start(raw[:, slot, :], adj[bass.ds(row, P), :]).then_inc(landed, 16)

            def row_of(i, c, hh):
                return ((i * CHUNKS + c) * 2 + hh) * P

            def user_of(n):
                if n < PASS1_RING and RING0[n] in ABOVE:
                    return above_ready, ABOVE.index(RING0[n]) + 1
                return lo_ready, SPLIT0.index(RING0[n]) + 1

            def load0(n):
                user, used = user_of(n - RING) if n >= RING else (None, None)
                above = n < PASS1_RING and RING0[n] in ABOVE
                load_unit(n % RING, row_of(*RING0[n]), user, used, raw_landed[n % RING], adj_rows if above else adj)

            sp.dma_start(x[:], x_in).then_inc(consts_landed, 16)
            sp.dma_start(w[:], w_in).then_inc(consts_landed, 16)
            sp.dma_start(bias[:], bias_in).then_inc(consts_landed, 16)
            n = 0
            for i in range(SLABS):
                while n < PASS1_RING and RING0[n][0] == i:
                    load0(n)
                    n += 1
                both = adj[row_of(i, LAST, 0):row_of(i, LAST, 0) + 2 * P, :].rearrange("(h p) n -> p h n", p=P)
                if i < LAST:
                    if i >= 1:
                        sp.wait_ge(lo_ready, SPLIT0.index((i - 1, i - 1, 1)) + 1)
                    sp.dma_start(res[:, i, :].rearrange("p (h n) -> p h n", h=2), both).then_inc(res_landed, 16)
                    both = adj[row_of(i, i, 0):row_of(i, i, 0) + 2 * P, :].rearrange("(h p) n -> p h n", p=P)
                    sp.dma_start(diag[:].rearrange("p (h n) -> p h n", h=2), both).then_inc(diag_landed, 16)
                else:
                    sp.dma_start(res[:, i, :].rearrange("p (h n) -> p h n", h=2), both).then_inc(res_landed, 16)
            for n in range(PASS1_RING, len(RING0)):
                load0(n)

            def body(layer, slab, chunks, parity=None):
                skip = 2 if layer == 1 else 0
                first = isinstance(slab, int) and slab == 0
                for r, (c, hh) in enumerate((c, hh) for c in chunks if c != LAST for hh in range(2)):
                    if r >= RING:
                        u = r - RING + (skip if first else 0)
                        user, used = lo_ready, split_index(layer, slab, u) + 1
                    elif first and layer == 1:
                        user, used = user_of(len(RING0) - RING + r)
                    else:
                        user, used = lo_ready, split_index(layer, slab, r + RING + skip) - UNITS_PER_SLAB + 1
                    load_unit(r % RING, slab * (CHUNKS * 2 * P) + (c * 2 + hh) * P, user, used, raw_landed[r % RING])

            for layer in range(1, LAYERS):
                slabs_of(sp, layer, body)

        @block.scalar
        def _(act):
            def split_hi(src, landed, value, g, slot):
                if landed is not None:
                    act.wait_ge(landed, value)
                if not isinstance(g, int) or g >= SPLIT:
                    act.wait_ge(unit_used, g - SPLIT + 1)
                nc.scalar.copy(hi[:, slot:slot + 1, :] if len(src.shape) == 3 else hi[:, slot, :], src).then_inc(hi_ready, 1)

            def free_acc(units, bank, dst):
                act.wait_ge(unit_used, units)
                nc.scalar.copy(dst, acc[bank][:]).then_inc(acc_free, 1)

            def squares(src, kind, at):
                for k in range(TILES):
                    last = nc.scalar.activation(junk_a[:, kind * TILES + k, :], src[:, k:k + 1, :], ACT.Square,
                                                accum_out=sq[:, kind, at + k:at + k + 1])
                return last

            def h_step(p, slab):
                act.wait_ge(ln_ready, p + 1)
                if not isinstance(p, int) or p >= 1:
                    act.wait_ge(h_turned, p)
                for k in range(TILES):
                    last = nc.scalar.activation(h[:, k:k + 1, :], rows(x, slab, k), ACT.Relu,
                                                bias=ln_bias[:, k:k + 1], scale=ln_scale[:, k:k + 1])
                last.then_inc(h_ready, 1)

            def hT_step(p):
                act.wait_ge(h_turned, p + 1)
                if not isinstance(p, int) or p >= 1:
                    act.wait_ge(m_ready, p)
                nc.scalar.copy(hT[:], h_ps[:]).then_inc(hT_ready, 1)

            def s_next_step(p, slab, seen):
                act.wait_ge(m_ready, p + 1)
                if seen is not None:
                    act.wait_ge(s_lo_ready, seen)
                nc.scalar.copy(rows(s_next, slab), m_ps[:]).then_inc(m_copied, 1)

            def split_s(layer, slab):
                m = layer * SLABS + place(layer, slab)
                if layer == 1:
                    act.wait_ge(hyp_done, place(layer, slab) + 1)
                else:
                    act.wait_ge(m_copied, m + 1)
                nc.scalar.copy(rows(s_hi, slab), rows(s_next, slab)).then_inc(s_hi_ready, 1)

            def after(n, slab, at, table, layer):
                p = n + SLABS
                if at == table.get("relu"):
                    q = n - SLABS
                    act.wait_ge(o_turned, n + 1)
                    act.wait_ge(h_turned, p)
                    act.wait_ge(hyp_pow, HYP_TO_POOL + q)
                    nc.scalar.activation(h[:], o_ps[:], ACT.Relu).then_inc(relu_ready, 1)
                    squares(o_ps, 0, 0)
                    act.wait_ge(relu_ready, 2 * q + 1)
                    squares(h, 1, 0).then_inc(relu_ready, 1)
                if at == table.get("tanh"):
                    act.wait_ge(hyp_to_act, HYP_TO_ACT + n - SLABS + 1)
                    nc.scalar.activation(hyp[:, 2, 0:TILES], hyp[:, 1, 0:TILES], ACT.Tanh).then_inc(post_tanh, 1)
                if at == table["h"]:
                    h_step(p, slab)
                if at == table["hT"]:
                    hT_step(p)
                if at == table["s_next"]:
                    s_next_step(p, slab, layer * SLABS)

            def scheduled(t):
                for name, n in SCHEDULE.get(t, []):
                    if name[:3] != "hyp":
                        p, slab = n + SLABS, LAST - n
                        half_at = next(slab - s0 for s0, width in GROUPS if s0 <= slab < s0 + width) * TILES
                        q = next(q for q, (s0, width) in enumerate(GROUPS) if s0 <= slab < s0 + width)
                    else:
                        q = n
                        w4 = GROUPS[q][1] * TILES
                        V = lambda i: hyp[:, i, 0:w4]
                    if name == "h":
                        h_step(p, slab)
                        if q >= 1:
                            act.wait_ge(hyp_to_pool, 2 * q - 1)
                        act.wait_ge(h_ready, p + 1)
                        squares(h, 0, half_at).then_inc(hyp_sq, 1)
                    if name == "hT":
                        hT_step(p)
                    if name == "s_next":
                        s_next_step(p, slab, SLABS)
                        act.wait_ge(m_copied, p + 1)
                        squares(rows(s_next, slab), 1, half_at).then_inc(hyp_sq, 1)
                    if name == "hyp2":
                        act.wait_ge(hyp_to_act, 3 * q + 1)
                        nc.scalar.activation(V(1), V(0), ACT.Ln, bias=1.0)
                        nc.scalar.activation(V(2), V(0), ACT.Ln, bias=1.0, scale=-1.0).then_inc(hyp_act, 1)
                    if name == "hyp3":
                        act.wait_ge(hyp_to_act, 3 * q + 2)
                        nc.scalar.activation(V(8), V(7), ACT.Tanh).then_inc(hyp_act, 1)
                    if name == "hyp5":
                        act.wait_ge(hyp_pow, 2 * q + 2)
                        nc.scalar.activation(V(20), V(18), ACT.Ln, bias=1.0)
                        nc.scalar.activation(V(21), V(16), ACT.Ln).then_inc(hyp_act, 1)
                    if name == "hyp6":
                        act.wait_ge(hyp_to_act, 3 * q + 3)
                        for k in range(w4):
                            sk = rows(s_next, GROUPS[q][0], k)
                            last = nc.scalar.activation(sk, sk, ACT.Copy, scale=hyp[:, 24, k:k + 1])
                        last.then_inc(hyp_act, 1)

            act.wait_ge(pool_consts, 2)
            nc.scalar.copy(ident_r[:], ident[:])
            nc.scalar.mul(mean_r[:], ones[:], 1.0 / P).then_inc(act_consts, 1)
            act.wait_ge(consts_landed, 48)
            nc.scalar.activation(junk_a[:, 0, :], bias[:, 1, :], ACT.Square, accum_out=bstat[:, 0:1]).then_inc(bias_step, 1)
            act.wait_ge(bias_step, 3)
            nc.scalar.activation(bstat[:, 4:5], bstat[:, 3:4], ACT.Tanh).then_inc(bias_tanh, 1)

            def prep0(i):
                h_step(i, i)
                hT_step(i)
                s_next_step(i, i, None)

            def split0(g):
                src, landed, value = source0(SPLIT0[g])
                split_hi(src, landed, value, g, g % SPLIT)

            prep0(0)
            g, above_n = 0, 0
            for i in range(SLABS + 1):
                below = 2 * i if i < SLABS else 0
                for _ in range(below - 2):
                    split0(g)
                    g += 1
                if i >= 1:
                    act.wait_ge(m_copied, i)
                    act.wait_ge(d_ready, i)
                    for k in range(TILES):
                        last = nc.scalar.activation(rows(s_hi, i - 1, k), rows(s_next, i - 1, k), ACT.Copy,
                                                    scale=d_of(i - 1, k))
                    last.then_inc(s_hi_ready, 1)
                    for _ in range(2):
                        split0(g)
                        g += 1
                    diag_units = g
                    for _ in range(min(below, 2)):
                        split0(g)
                        g += 1
                if i < SLABS - 1:
                    h_step(i + 1, i + 1)
                units = [u for u in ABOVE if u[0] == i]
                for k in range(max(len(units), 4)):
                    if k == 2 and i < SLABS - 1:
                        hT_step(i + 1)
                    if k < len(units):
                        _, c, hh = units[k]
                        n = RING0.index(units[k])
                        act.wait_ge(raw_landed[n % RING], 16 * (n // RING + 1))
                        for e in range(2):
                            half_unit = raw[:, n % RING, e * SLAB:(e + 1) * SLAB]
                            last = nc.scalar.activation(half_unit, half_unit, ACT.Copy,
                                                        accum_out=above[:, i % 2, 2 * hh + e, c:c + 1])
                        last.then_inc(above_ready, 1)
                if i < SLABS - 1:
                    s_next_step(i + 1, i + 1, None)
                if i >= 1:
                    act.wait_ge(s_lo_ready, i)
                    free_acc(diag_units, (i - 1) % 2, rows(s_next, i - 1).rearrange("p t f -> p (t f)"))

            for u in range(PASS2):
                split0(PASS1_SPLIT + u)
                scheduled(u)

            def body(layer, slab, chunks, parity=None):
                first = isinstance(slab, int) and slab == 0
                if isinstance(slab, int):
                    parity = slab % 2
                n = layer * SLABS + slab - 1
                prev, lay = (LAST, layer) if first else (slab - 1, layer + 1)
                for u in range(UNITS_PER_SLAB):
                    if first and u % 2 == 0:
                        split_s(layer, chunks[u // 2])
                    src, landed, value = source(layer, slab, u, chunks)
                    split_hi(src, landed, value, split_index(layer, slab, u), u % SPLIT)
                    if first and layer == 1:
                        scheduled(PASS2 + u)
                        continue
                    if u == 3:
                        act.wait_ge(o_turned, n)
                        free_acc(split_index(layer, slab, 0), parity, o_sb[:])
                    if lay < LAYERS:
                        after(n, prev, u, table(layer, slab), lay)
                    elif u == AT["h"]:
                        send(n, prev)

            def send(n, slab):
                act.wait_ge(x_ready, n + 1)
                act.dma_start(out[:, bass.ds(slab * TILES, TILES), :], rows(x, slab)).then_inc(out_landed, 16)

            for layer in range(1, LAYERS):
                slabs_of(act, layer, body)
            n = LAYERS * SLABS - 1
            act.wait_ge(o_turned, n)
            free_acc(split_index(LAYERS, 0, 0), (evac_index(LAYERS, 0) - 1) % 2, o_sb[:])
            send(n, LAST)
            act.wait_ge(out_landed, 16 * SLABS)

        @block.vector
        def _(dve):
            steps = {}

            def link(s, ins, base=0):
                steps[s.name] = steps.get(s.name, 0) + 1
                ins.then_inc(s, 1)
                dve.wait_ge(s, base + steps[s.name])

            def split_lo(src, g, slot):
                dve.wait_ge(hi_ready, g + 1)
                flat = len(src.shape) == 2
                hs = hi[:, slot, :] if flat else hi[:, slot:slot + 1, :]
                ls = lo[:, slot, :] if flat else lo[:, slot:slot + 1, :]
                last = nc.vector.tensor_tensor(ls, src, hs.bitcast(FP32), ALU.subtract)
                last.then_inc(lo_ready, 1)
                return last

            def x_step(n, slab, layer):
                src = layer - 1
                base = (n - src * SLABS) * LINKS[src]
                if src != 1:
                    steps[post_step[src].name] = 0
                dve.wait_ge(o_turned, n + 1)
                xs = rows(x, slab)
                if src in (0, 2):
                    dve.wait_ge(h_turned, n + SLABS)
                    if src == 0 and n >= 1:
                        dve.wait_ge(hyp_sq, 2 * n - 1)
                    for k in range(TILES):
                        last = nc.vector.scalar_tensor_tensor(h[:, k:k + 1, :], o_ps[:, k:k + 1, :], d_of(slab, k),
                                                              bias[:, src:src + 1, :], ALU.mult, ALU.add)
                    link(post_step[src], last, base)
                    if src == 0:
                        last = nc.vector.scalar_tensor_tensor(xs, h[:], 0.0, xs, ALU.max, ALU.add)
                    else:
                        last = nc.vector.tensor_tensor(xs, h[:], xs, ALU.add)
                if src == 3:
                    last = nc.vector.scalar_tensor_tensor(xs, o_ps[:], 0.0, xs, ALU.max, ALU.add)
                if src == 1:
                    q = n - SLABS
                    st = post_step[1]
                    g, vn, rv, out_scale = (hyp[:, r, 0:TILES] for r in (6, 1, 8, 11))
                    dve.wait_ge(post_tanh, q + 1)
                    steps[st.name] = 4
                    link(st, nc.vector.scalar_tensor_tensor(hyp[:, 9, 0:TILES], hyp[:, 2, 0:TILES], MAXNORM, rv,
                                                            ALU.min, ALU.mult), base)
                    link(st, nc.vector.tensor_tensor(out_scale, hyp[:, 9, 0:TILES], g, ALU.mult), base)
                    for k in range(TILES):
                        xk = rows(x, slab, k)
                        last = nc.vector.scalar_tensor_tensor(xk, h[:, k:k + 1, :], hyp[:, 11, k:k + 1], xk,
                                                              ALU.mult, ALU.add)
                last.then_inc(x_ready, 1)
                assert steps[post_step[src].name] == LINKS[src], steps

            def carry_wait():
                nc.vector.memset(spare[:], 0.0)

            def post1_step(n):
                dve.wait_ge(relu_ready, 2 * (n - SLABS) + 2)
                nc.vector.tensor_scalar(sq[:, :, 0:TILES], sq[:, :, 0:TILES], TINY2, None,
                                        ALU.max).then_inc(hyp_to_pool, 1)

            def post2_step(n):
                q, st = n - SLABS, post_step[1]
                base = q * LINKS[1]
                steps[st.name] = 0
                un, rn = nrm[:, 0, 0:TILES], nrm[:, 1, 0:TILES]
                iu, g, v, vn, rv = (hyp[:, r, 0:TILES] for r in (4, 6, 7, 1, 8))
                dve.wait_ge(hyp_pow, HYP_TO_POOL + q + 1)
                link(st, nc.vector.reciprocal(iu, un), base)
                link(st, nc.vector.scalar_tensor_tensor(g, un, ATANH_MAX, iu, ALU.min, ALU.mult), base)
                link(st, nc.vector.tensor_tensor(v, g, rn, ALU.mult), base)
                nc.vector.tensor_scalar(vn, v, TINY, None, ALU.max).then_inc(hyp_to_act, 1)
                dve.wait_ge(hyp_to_act, HYP_TO_ACT + q + 1)
                link(st, nc.vector.reciprocal(rv, vn), base)

            def stats_step(p, slab, xr):
                if xr is not None:
                    dve.wait_ge(x_ready, xr)
                    carry_wait()
                for k in range(TILES):
                    last = nc.vector.bn_stats(stats[:, k, :], rows(x, slab, k))
                last.then_inc(stats_ready, 1)
                dve.wait_ge(stats_ready, p + 1)
                carry_wait()
                for k in range(TILES):
                    last = nc.vector.bn_aggr(mv[:, k, :], stats[:, k, :])
                last.then_inc(mv_ready, 1)
                dve.wait_ge(mv_ready, p + 1)
                nc.vector.tensor_scalar(var_eps[:], mv[:, :, 1], LN_EPS, None, ALU.add).then_inc(var_ready, 1)

            def ln_step(p, slab, layer):
                dve.wait_ge(rstd_ready, p + 1)
                if not isinstance(p, int) or p >= 1:
                    dve.wait_ge(h_ready, p)
                if layer == 2:
                    nc.vector.tensor_tensor(ln_scale[:], rstd[:], d_of(slab), ALU.mult).then_inc(scale_ready, 1)
                else:
                    nc.vector.tensor_copy(ln_scale[:], rstd[:]).then_inc(scale_ready, 1)
                dve.wait_ge(scale_ready, p + 1)
                nc.vector.scalar_tensor_tensor(ln_bias[:], mv[:, :, 0], -1.0, ln_scale[:], ALU.mult,
                                               ALU.mult).then_inc(ln_ready, 1)

            done = {"steps": 0, "seen": 0}

            def do(ins):
                ins.then_inc(hyp_step, 1)
                done["steps"] += 1
                return done["steps"]

            def needs(step):
                if step > done["seen"]:
                    dve.wait_ge(hyp_step, step)
                    done["seen"] = step

            def tt(o, a, b, op, need=0):
                needs(need)
                return do(nc.vector.tensor_tensor(o, a, b, op))

            def ts(o, a, s1, op0, need=0, s2=None, op1=None):
                needs(need)
                return do(nc.vector.tensor_scalar(o, a, s1, s2, op0, *([] if op1 is None else [op1])))

            def stt(o, a, s, b, op0, op1, need=0):
                needs(need)
                return do(nc.vector.scalar_tensor_tensor(o, a, s, b, op0, op1))

            def hyper(q, step):
                slab, width = GROUPS[q]
                w4 = width * TILES
                V = lambda i: hyp[:, i, 0:w4]
                h_norm, m_norm = nrm[:, 0, 0:w4], nrm[:, 1, 0:w4]
                if step == 1:
                    dve.wait_ge(hyp_sq, 2 * (LAST - slab) + 2)
                    for k in range(w4):
                        last = nc.vector.scalar_tensor_tensor(junk_v[:, k, :], rows(s_next, slab, k), 1.0, hyp_b[:],
                                                              ALU.mult, ALU.mult, accum_out=hyp[:, 3, k:k + 1])
                    do(last)
                    nc.vector.tensor_scalar(hyp[:, 4:6, 0:w4], sq[:, :, 0:w4], TINY2, None,
                                            ALU.max).then_inc(hyp_to_pool, 1)
                if step == 2:
                    dve.wait_ge(hyp_pow, 2 * q + 1)
                    nc.vector.tensor_scalar(V(0), h_norm, CLIP, None, ALU.min).then_inc(hyp_to_act, 1)
                    a = ts(V(12), V(4), SERIES[0], ALU.mult)
                    do(nc.vector.reciprocal(hyp[:, 9:11, 0:w4], nrm[:, :, 0:w4]))
                    for coef in SERIES[1:]:
                        a = stt(V(12), V(12), coef, V(4), ALU.add, ALU.mult, need=a)
                    ts(V(11), V(12), 1.0, ALU.add, need=a)
                if step == 3:
                    needs(done["steps"])
                    dve.wait_ge(hyp_act, 4 * q + 1)
                    a = tt(V(13), V(1), V(2), ALU.subtract)
                    a = stt(V(14), V(13), 0.5, V(9), ALU.mult, ALU.mult, need=a)
                    a = tt(V(12), V(11), V(14), ALU.subtract, need=a)
                    a = stt(V(12), h_norm, SERIES_BELOW, V(12), ALU.is_lt, ALU.mult, need=a)
                    a = tt(V(13), V(12), V(14), ALU.add, need=a)
                    needs(a)
                    nc.vector.tensor_tensor(V(7), V(13), m_norm, ALU.mult).then_inc(hyp_to_act, 1)
                if step == 4:
                    y2, one_y2 = bstat[:, 8:9], bstat[:, 9:10]
                    dve.wait_ge(hyp_act, 4 * q + 2)
                    a = stt(V(11), V(8), MAXNORM, V(10), ALU.min, ALU.mult)
                    b = tt(V(13), V(11), V(3), ALU.mult, need=a)
                    a = tt(V(12), V(11), V(11), ALU.mult)
                    b = ts(V(14), V(13), 2.0, ALU.mult, b, 1.0, ALU.add)
                    a = tt(V(15), V(12), V(5), ALU.mult, need=a)
                    b = stt(V(19), V(14), y2, V(11), ALU.add, ALU.mult, need=b)
                    c = stt(V(13), V(15), y2, V(14), ALU.mult, ALU.add, need=a)
                    a = ts(V(12), V(15), -1.0, ALU.mult, a, 1.0, ALU.add)
                    c = ts(V(22), V(13), TINY, ALU.max, need=c)
                    needs(c)
                    c = do(nc.vector.reciprocal(V(23), V(22)))
                    a = tt(V(14), V(19), V(23), ALU.mult, need=c)
                    b = tt(V(15), V(12), V(23), ALU.mult)
                    stt(V(16), V(12), one_y2, V(23), ALU.mult, ALU.mult)
                    c = tt(V(13), V(14), V(3), ALU.mult, need=a)
                    b = ts(V(19), V(15), y2, ALU.mult, need=b)
                    a = tt(V(22), V(14), V(14), ALU.mult)
                    b = stt(V(27), V(13), 2.0, V(19), ALU.mult, ALU.add, need=b)
                    a = tt(V(28), V(22), V(5), ALU.mult, need=a)
                    b = tt(V(29), V(27), V(15), ALU.mult, need=b)
                    a = tt(V(30), V(29), V(28), ALU.add, need=b)
                    needs(a)
                    nc.vector.tensor_scalar(V(17), V(30), TINY2, None, ALU.max).then_inc(hyp_to_pool, 1)
                    dve.wait_ge(hyp_to_pool, 2 * q + 2)
                    a = ts(V(12), V(17), SERIES[0], ALU.mult)
                    for coef in SERIES[1:]:
                        a = stt(V(12), V(12), coef, V(17), ALU.add, ALU.mult, need=a)
                    ts(V(11), V(12), 1.0, ALU.add, need=a)
                if step == 5:
                    needs(done["steps"])
                    dve.wait_ge(hyp_pow, 2 * q + 2)
                    c = do(nc.vector.reciprocal(V(19), V(18)))
                    dve.wait_ge(hyp_act, 4 * q + 3)
                    a = stt(V(22), V(21), -0.5, V(20), ALU.mult, ALU.add)
                    a = stt(V(23), V(22), ATANH_MAX, V(19), ALU.min, ALU.mult, need=a)
                    b = tt(V(12), V(11), V(23), ALU.subtract, need=a)
                    b = stt(V(13), V(18), SERIES_BELOW, V(12), ALU.is_lt, ALU.mult, need=b)
                    b = tt(V(22), V(13), V(23), ALU.add, need=b)
                    tt(V(25), V(22), V(15), ALU.mult, need=b)
                    nc.vector.tensor_tensor(V(24), V(22), V(14), ALU.mult).then_inc(hyp_to_act, 1)
                if step == 6:
                    needs(done["steps"])
                    dve.wait_ge(hyp_act, 4 * q + 4)
                    for k in range(w4):
                        sk = rows(s_next, slab, k)
                        last = nc.vector.scalar_tensor_tensor(sk, hyp_b[:], hyp[:, 25, k:k + 1], sk, ALU.mult, ALU.add)
                        if k % TILES == TILES - 1:
                            last.then_inc(hyp_done, 1)

            def scheduled(t):
                for name, n in SCHEDULE.get(t, []):
                    if name == "x":
                        x_step(n, LAST - n, 1)
                        stats_step(n + SLABS, LAST - n, n + 1)
                    if name == "ln":
                        ln_step(n + SLABS, LAST - n, 1)
                    if name[:3] == "hyp":
                        hyper(n, int(name[3]))

            def after(n, slab, at, table, layer):
                p = n + SLABS
                if at == table.get("post1"):
                    post1_step(n)
                if at == table.get("post2"):
                    post2_step(n)
                if at == table["x"]:
                    x_step(n, slab, layer)
                    if layer < LAYERS:
                        stats_step(p, slab, n + 1)
                if layer < LAYERS and at == table["ln"]:
                    ln_step(p, slab, layer)

            def split_s(layer, slab):
                m = layer * SLABS + place(layer, slab)
                dve.wait_ge(s_hi_ready, m + 1)
                nc.vector.tensor_tensor(rows(s_lo, slab), rows(s_next, slab), rows(s_hi, slab).bitcast(FP32),
                                        ALU.subtract).then_inc(s_lo_ready, 1)

            nc.vector.memset(half[:], 0.5)
            nc.vector.memset(minus_half[:], -0.5).then_inc(dve_consts, 1)
            dve.wait_ge(bias_step, 1)
            nc.vector.tensor_scalar(bstat[:, 1:2], bstat[:, 0:1], TINY2, None, ALU.max).then_inc(bias_step, 1)
            dve.wait_ge(bias_pow, 1)
            nc.vector.tensor_scalar(bstat[:, 3:4], bstat[:, 2:3], 1.0, None, ALU.mult).then_inc(bias_step, 1)
            dve.wait_ge(bias_step, 3)
            nc.vector.reciprocal(bstat[:, 5:6], bstat[:, 3:4]).then_inc(bias_step, 1)
            dve.wait_ge(bias_tanh, 1)
            nc.vector.tensor_scalar(bstat[:, 6:7], bstat[:, 4:5], MAXNORM, None, ALU.min).then_inc(bias_step, 1)
            dve.wait_ge(bias_step, 5)
            nc.vector.tensor_tensor(bstat[:, 7:8], bstat[:, 6:7], bstat[:, 5:6], ALU.mult).then_inc(bias_step, 1)
            dve.wait_ge(bias_step, 6)
            nc.vector.tensor_scalar(hyp_b[:, 0, :], bias[:, 1, :], bstat[:, 7:8], None, ALU.mult).then_inc(bias_step, 1)
            dve.wait_ge(bias_step, 7)
            nc.vector.scalar_tensor_tensor(junk_v[:, 0, :], hyp_b[:, 0, :], 1.0, hyp_b[:, 0, :], ALU.mult, ALU.mult,
                                           accum_out=bstat[:, 8:9]).then_inc(bias_step, 1)
            dve.wait_ge(bias_step, 8)
            nc.vector.tensor_scalar(bstat[:, 9:10], bstat[:, 8:9], -1.0, 1.0, ALU.mult, ALU.add).then_inc(bias_step, 1)
            dve.wait_ge(bias_step, 9)

            dve.wait_ge(consts_landed, 48)
            stats_step(0, 0, None)
            ln_step(0, 0, 0)
            g = 0

            def add_rows(src, landed, value, fresh=False, final=False):
                dve.wait_ge(landed, value)
                a, b = src[:, 0:SLAB], src[:, SLAB:UNIT]
                if fresh:
                    link(row_step, nc.vector.tensor_tensor(row_part[:], a, b, ALU.add))
                    return
                link(row_step, nc.vector.tensor_tensor(row_part[:], row_part[:], a, ALU.add))
                last = nc.vector.tensor_tensor(row_part[:], row_part[:], b, ALU.add)
                if final:
                    last.then_inc(rows_summed, 1)
                else:
                    link(row_step, last)

            def split0(g):
                src, _, _ = source0(SPLIT0[g])
                split_lo(src, g, g % SPLIT)

            for i in range(SLABS + 1):
                below = 2 * i if i < SLABS else 0
                for _ in range(below - 2):
                    split0(g)
                    g += 1
                if i < SLABS - 1:
                    stats_step(i + 1, i + 1, None)
                if i >= 1:
                    dve.wait_ge(s_hi_ready, i)
                    for k in range(TILES):
                        last = nc.vector.scalar_tensor_tensor(rows(s_lo, i - 1, k), rows(s_next, i - 1, k), d_of(i - 1, k),
                                                              rows(s_hi, i - 1, k).bitcast(FP32), ALU.mult, ALU.subtract)
                    last.then_inc(s_lo_ready, 1)
                    for _ in range(2 + min(below, 2)):
                        split0(g)
                        g += 1
                if i < SLABS - 1:
                    ln_step(i + 1, i + 1, 0)
                if i < SLABS:
                    for hh in range(2):
                        add_rows(res[:, i, hh * UNIT:(hh + 1) * UNIT], res_landed, 16 * (i + 1), fresh=hh == 0)
                    if i < LAST:
                        for hh in range(2):
                            add_rows(diag[:, hh * UNIT:(hh + 1) * UNIT], diag_landed, 16 * (i + 1),
                                     final=i == 0 and hh == 1)
                    if i >= 1:
                        dve.wait_ge(unit_used, g)
                        nc.vector.tensor_tensor(row_part[:], row_part[:], row_ps[:], ALU.add).then_inc(rows_summed, 1)
                    count = LAST - 1 - i
                    if count > 0:
                        dve.wait_ge(above_ready, sum(2 * (LAST - 1 - k) for k in range(i + 1)))
                        nc.vector.tensor_reduce(above_sum[:], above[:, i % 2, :, i + 1:LAST], mybir.AxisListType.X,
                                                ALU.add).then_inc(above_summed, 1)
                        dve.wait_ge(above_summed, i + 1)
                    dve.wait_ge(deg_ready, i + 1)
                    if count > 0:
                        nc.vector.scalar_tensor_tensor(deg1[:], deg_ps[:], 1.0, above_sum[:], ALU.add,
                                                       ALU.add).then_inc(deg1_ready, 1)
                    else:
                        nc.vector.tensor_scalar(deg1[:], deg_ps[:], 1.0, None, ALU.add).then_inc(deg1_ready, 1)

            def second_unit(gg):
                split0(gg)
                for e in range(SLABS, EVACS0 - 1):
                    slab = SLABS - 2 - (e - SLABS)
                    end = PASS1_SPLIT + (LAST - slab) * (SLABS - slab)
                    if gg == end + SPLIT - 2:
                        join(e, slab, end)

            def join(e, slab, units):
                dve.wait_ge(unit_used, units)
                part = rows(s_next, slab).rearrange("p t f -> p (t f)")
                nc.vector.tensor_tensor(part, part, acc[e % 2][:], ALU.add).then_inc(acc_free, 1)

            dve.wait_ge(acc_free, SLABS)
            for u in range(PASS2):
                second_unit(PASS1_SPLIT + u)
                scheduled(u)

            def body(layer, slab, chunks, parity=None):
                n = layer * SLABS + slab - 1
                first = isinstance(slab, int) and slab == 0
                prev, lay = (LAST, layer) if first else (slab - 1, layer + 1)
                for u in range(UNITS_PER_SLAB):
                    if first and u % 2 == 0:
                        split_s(layer, chunks[u // 2])
                    src, _, value = source(layer, slab, u, chunks)
                    split_lo(src, split_index(layer, slab, u), u % SPLIT)
                    if first and layer == 1:
                        if u == 2:
                            join(EVACS0 - 1, 0, len(SPLIT0))
                        scheduled(PASS2 + u)
                    else:
                        after(n, prev, u, table(layer, slab), lay)

            for layer in range(1, LAYERS):
                slabs_of(dve, layer, body)
            after(LAYERS * SLABS - 1, LAST, AT["x"], AT, LAYERS)

        @block.tensor
        def _(pe):
            def contract(bank, c, hh, slot, first, last_unit, g, rowsum=None):
                pe.wait_ge(lo_ready, g + 1)
                for t in range(2):
                    j = c * TILES + hh * 2 + t
                    a, b = hi[:, slot, t * SLAB:(t + 1) * SLAB], lo[:, slot, t * SLAB:(t + 1) * SLAB]
                    nc.tensor.matmul(acc[bank][:], s_hi[:, j, :], a, start=first and t == 0, stop=False)
                    nc.tensor.matmul(acc[bank][:], s_hi[:, j, :], b, start=False, stop=False)
                    last = nc.tensor.matmul(acc[bank][:], s_lo[:, j, :], a, start=False, stop=last_unit and t == 1)
                if rowsum is not None:
                    for t in range(2):
                        for k, part in enumerate((hi, lo)):
                            last = nc.tensor.matmul(row_ps[:], mean_r[:], part[:, slot, t * SLAB:(t + 1) * SLAB],
                                                    start=rowsum == 0 and t + k == 0, stop=rowsum == 2 and t + k == 2)
                last.then_inc(unit_used, 1)
                return last

            def turn_o(n, slab, own, src):
                pe.wait_ge(x_ready, n) if not isinstance(n, int) or n >= 1 else None
                for k in range(TILES):
                    last = nc.tensor.matmul(o_ps[:, k, :], src(k), ident[:], is_transpose=True, start=k == 0,
                                            stop=(not own) and k == TILES - 1)
                if own:
                    flat = o_ps[:].rearrange("p t f -> p (t f)")
                    nc.tensor.matmul(flat, ident_r[:], rows(s_hi, slab).rearrange("p t f -> p (t f)"), start=False, stop=False)
                    last = nc.tensor.matmul(flat, ident_r[:], rows(s_lo, slab).rearrange("p t f -> p (t f)"), start=False, stop=True)
                last.then_inc(o_turned, 1)

            def turn_h(p):
                pe.wait_ge(h_ready, p + 1)
                if not isinstance(p, int) or p >= 1:
                    pe.wait_ge(hT_ready, p)
                for k in range(TILES):
                    last = nc.tensor.matmul(h_ps[:, k * P:(k + 1) * P], h[:, k, :], ident[:], is_transpose=True,
                                            start=k == 0, stop=k == TILES - 1)
                last.then_inc(h_turned, 1)

            def times_w(p, layer):
                pe.wait_ge(hT_ready, p + 1)
                if not isinstance(p, int) or p >= 1:
                    pe.wait_ge(m_copied, p)
                for k in range(TILES):
                    last = nc.tensor.matmul(m_ps[:, k, :], hT[:, k * P:(k + 1) * P], w[:, layer, :],
                                            start=k == 0, stop=k == TILES - 1)
                last.then_inc(m_ready, 1)

            def after(n, slab, at, table, layer):
                if at == table["turn_o"]:
                    pe.wait_ge(acc_free, EVACS0 - SLABS + n + 1)
                    turn_o(n, slab, layer == 3, lambda k: o_sb[:, k * P:(k + 1) * P])
                if layer < LAYERS and at == table["turn_h"]:
                    turn_h(n + SLABS)
                if layer < LAYERS and at == table["times_w"]:
                    times_w(n + SLABS, layer)

            def scheduled(t):
                for name, n in SCHEDULE.get(t, []):
                    slab = LAST - n
                    if name == "turn_o":
                        pe.wait_ge(acc_free, SLABS + n)
                        turn_o(n, slab, True, lambda k: s_next[:, slab * TILES + k, :])
                    if name == "turn_h":
                        turn_h(n + SLABS)
                    if name == "times_w":
                        times_w(n + SLABS, 1)

            pe.wait_ge(pool_consts, 2)
            pe.wait_ge(consts_landed, 48)
            turn_h(0)
            times_w(0, 0)
            pe.wait_ge(act_consts, 1)
            g = 0
            for i in range(SLABS + 1):
                below = 2 * i if i < SLABS else 0
                if below:
                    if i >= 2:
                        pe.wait_ge(acc_free, i - 1)
                        pe.wait_ge(rows_summed, i)

                def unit_below(u, g):
                    contract(i % 2, u // 2, u % 2, g % SPLIT, u == 0, False, g,
                             rowsum=0 if u == 0 else 2 if u == below - 1 else 1)

                for u in range(below - 2):
                    unit_below(u, g)
                    g += 1
                if i >= 1:
                    pe.wait_ge(s_lo_ready, i)
                    for hh in range(2):
                        contract((i - 1) % 2, i - 1, hh, g % SPLIT, i == 1 and hh == 0, hh == 1, g)
                        g += 1
                if below:
                    for u in range(below - 2, below):
                        unit_below(u, g)
                        g += 1
                if i < SLABS - 1:
                    turn_h(i + 1)
                    times_w(i + 1, 0)
                if i < SLABS:
                    pe.wait_ge(rows_summed, i + 1)
                    if i >= 1:
                        pe.wait_ge(deg1_ready, i)
                    for k in range(TILES):
                        last = nc.tensor.matmul(deg_ps[:, k:k + 1], row_part[:, k * P:(k + 1) * P], ones[:, 0:1],
                                                start=k == 0, stop=k == TILES - 1)
                    last.then_inc(deg_ready, 1)

            def second_unit(gg):
                i, c, hh = SPLIT0[gg]
                e = SLABS + (SLABS - 2 - i)
                if c == LAST and hh == 0:
                    pe.wait_ge(acc_free, e - 1)
                end = c == i + 1 and hh == 1
                contract(e % 2, c, hh, gg % SPLIT, c == LAST and hh == 0, end, gg)

            for u in range(PASS2):
                second_unit(PASS1_SPLIT + u)
                scheduled(u)

            def body(layer, slab, chunks, parity=None):
                if isinstance(slab, int):
                    parity = slab % 2
                bank = 1 - parity
                first = isinstance(slab, int) and slab == 0
                n = layer * SLABS + slab - 1
                prev, lay = (LAST, layer) if first else (slab - 1, layer + 1)
                pe.wait_ge(acc_free, evac_index(layer, slab) - 1)
                for u in range(UNITS_PER_SLAB):
                    c = chunks[u // 2]
                    if first and u % 2 == 0:
                        pe.wait_ge(s_lo_ready, layer * SLABS + u // 2 + 1)
                    contract(bank, c, u % 2, u % SPLIT, u == 0, u == UNITS_PER_SLAB - 1, split_index(layer, slab, u))
                    if first and layer == 1:
                        scheduled(PASS2 + u)
                    else:
                        after(n, prev, u, table(layer, slab), lay)

            for layer in range(1, LAYERS):
                slabs_of(pe, layer, body)
            after(LAYERS * SLABS - 1, LAST, AT["turn_o"], AT, LAYERS)

        @block.gpsimd
        def _(pool):
            nc.gpsimd.memset(ones[:], 1.0).then_inc(pool_consts, 1)
            pool.wait_ge(pool_consts, 1)
            nc.gpsimd.affine_select(out=ident[:], in_=ones[:], compare_op=ALU.is_equal, fill=0.0, base=0,
                                    pattern=[[-1, P]], channel_multiplier=1).then_inc(pool_consts, 1)
            pool.wait_ge(dve_consts, 1)
            pool.wait_ge(bias_step, 2)
            nc.gpsimd.tensor_tensor(bstat[:, 2:3], bstat[:, 1:2], half[:, 0, 0:1], ALU.pow).then_inc(bias_pow, 1)

            def rstd_step(p):
                pool.wait_ge(var_ready, p + 1)
                nc.gpsimd.tensor_tensor(rstd[:], var_eps[:], minus_half[:], ALU.pow).then_inc(rstd_ready, 1)

            rstd_step(0)
            for i in range(SLABS):
                if i < SLABS - 1:
                    rstd_step(i + 1)
                pool.wait_ge(deg1_ready, i + 1)
                nc.gpsimd.tensor_tensor(d_of(i), deg1[:], minus_half[:], ALU.pow).then_inc(d_ready, 1)
            for t in sorted(SCHEDULE):
                for name, n in SCHEDULE[t]:
                    if name == "x":
                        rstd_step(n + SLABS)
                    if name == "hyp1":
                        w4 = GROUPS[n][1] * TILES
                        pool.wait_ge(hyp_to_pool, 2 * n + 1)
                        nc.gpsimd.tensor_tensor(nrm[:, :, 0:w4], hyp[:, 4:6, 0:w4], half[:, :, 0:w4],
                                                ALU.pow).then_inc(hyp_pow, 1)
                    if name == "hyp4":
                        w4 = GROUPS[n][1] * TILES
                        pool.wait_ge(hyp_to_pool, 2 * n + 2)
                        nc.gpsimd.tensor_tensor(hyp[:, 18, 0:w4], hyp[:, 17, 0:w4], half[:, 0, 0:w4],
                                                ALU.pow).then_inc(hyp_pow, 1)
            with pool.Fori(0, SLABS) as it:
                pool.wait_ge(hyp_to_pool, it + HYP_TO_POOL + 1)
                nc.gpsimd.tensor_tensor(nrm[:, :, 0:TILES], sq[:, :, 0:TILES], half[:, :, 0:TILES],
                                        ALU.pow).then_inc(hyp_pow, 1)
                rstd_step(it + 2 * SLABS)
            with pool.Fori(0, SLABS) as it:
                rstd_step(it + 3 * SLABS)


def kernel(x, adj, L0_gnn_W, L0_gnn_b, L1_gnn_weight, L1_gnn_bias, L2_gnn_W, L2_gnn_b, L3_gnn_weights):
    import numpy as np
    import concourse.bacc as bacc
    from concourse.bass_utils import run_bass_kernel_spmd

    a = np.asarray(adj).reshape(SLABS, SLAB, CHUNKS, 2, 2, P).transpose(0, 2, 3, 5, 4, 1)
    b = np.asarray(adj).reshape(SLABS, 2, 2, P, CHUNKS, SLAB).transpose(0, 4, 1, 3, 2, 5)
    arrays = {
        "adj_units": np.ascontiguousarray(a).reshape(SLABS * CHUNKS * 2 * P, UNIT),
        "adj_row_units": np.ascontiguousarray(b).reshape(SLABS * CHUNKS * 2 * P, UNIT),
        "x_rows": np.ascontiguousarray(np.asarray(x).reshape(N // P, P, F).transpose(1, 0, 2)),
        "weights": np.ascontiguousarray(np.stack([np.asarray(L0_gnn_W), np.asarray(L1_gnn_weight).T,
                                                  np.asarray(L2_gnn_W).T, np.asarray(L3_gnn_weights)], axis=1)),
        "biases": np.ascontiguousarray(np.broadcast_to(
            np.stack([np.asarray(L0_gnn_b), np.asarray(L1_gnn_bias), np.asarray(L2_gnn_b)]), (P, 3, F))),
    }
    nc = bacc.Bacc("TRN2", target_bir_lowering=False, num_devices=1,
                   dynamic_dma_scratch_size=4096)
    aps = [nc.dram_tensor(k, v.shape, FP32, kind="ExternalInput").ap() for k, v in arrays.items()]
    out = nc.dram_tensor("out_rows", (P, N // P, F), FP32, kind="ExternalOutput").ap()
    build(nc, *aps, out)
    r = run_bass_kernel_spmd(nc, [arrays], core_ids=[0])
    got = r.results[0]["out_rows"]
    return np.ascontiguousarray(got.transpose(1, 0, 2)).reshape(N, F)
```

```python
import concourse.bass as bass
from concourse import mybir
from contextlib import ExitStack

FP32 = mybir.dt.float32
FP32R = mybir.dt.float32r
ALU = mybir.AluOpType
ACT = mybir.ActivationFunctionType

N = 4096
F = 128
P = 128
LAYERS = 4
SLAB = 512
SLABS = N // SLAB
TILES = SLAB // P
CHUNKS = N // SLAB
UNIT = 2 * SLAB
LAST = CHUNKS - 1
RING = 7
SPLIT = 4
RING_PER_SLAB = 2 * LAST
UNITS_PER_SLAB = 2 * CHUNKS

LN_EPS = 1e-5
TINY = 1e-15
TINY2 = TINY * TINY
ABOVE_ZERO = 1e-37
MAXNORM = 1.0 - 1e-5
CLIP = 1.0 - 1e-7
ATANH_MAX = 6.1030338227611125
SERIES_BELOW = 0.25
SERIES = [1.0 / 11, 1.0 / 9, 1.0 / 7, 1.0 / 5, 1.0 / 3]


SECOND = [4, 6, 5, 3, 2, 1, 0]
STEPS_AT = {0: ["stats"], 1: ["sum"], 2: ["turn_deg"], 4: ["deg1"], 5: ["rows"], 7: ["h", "scale", "own", "own"],
            8: ["turn_h"], 9: ["own_rows"], 11: ["hT", "times_w", "evac"], 13: ["s_next"]}
LAST_STEP = 13


def first_pass(i):
    below = [(i, c, h) for c in range(i - 1) for h in range(2)] if i < SLABS else []
    late = [(i, i - 1, h) for h in range(2)] if 0 < i < SLABS else []
    above = [(i, c, h) for c in range(i + 1, LAST) for h in range(2)]
    steps, pos, own, turn = [], 0, 0, 0
    while pos <= LAST_STEP or below or late or above:
        for name in STEPS_AT.get(pos, []):
            if name in ("stats", "h", "turn_h", "hT", "times_w", "s_next") and i >= SLABS - 1:
                continue
            if name in ("sum", "turn_deg", "deg1", "scale", "own", "evac") and i == 0:
                continue
            if name == "rows" and i == SLABS or name == "own_rows" and i >= LAST:
                continue
            unit = None
            if name == "own":
                unit, own = (i - 1, i - 1, own), own + 1
            steps.append((name, unit))
        mine = late if pos >= 7 and late else below
        if i == SLABS and 2 <= pos < 6:
            steps.append(("second", (SECOND[0], LAST - 1 - (pos - 2) // 2, pos % 2)))
        if mine and (turn == 0 or not above):
            steps.append(("below", mine.pop(0)))
        elif above:
            steps.append(("above", above.pop(0)))
        elif mine:
            steps.append(("below", mine.pop(0)))
        turn = 1 - turn
        pos += 1
    return steps


FIRST_PASS = [first_pass(i) for i in range(SLABS + 1)]


def rows_by_vector():
    units = []
    for i in range(SLABS - 3, SLABS):
        after = FIRST_PASS[i][FIRST_PASS[i].index(("rows", None)):]
        units += [u for name, u in after if name == "below" and u[2] == 1 and u[1] < i - 1]
    return units


ROWS_BY_VECTOR = rows_by_vector()


def ring_order():
    units = [u for steps in FIRST_PASS for name, u in steps if name in ("below", "above")]
    for i in SECOND:
        units += [(i, c, h) for c in range(LAST - 1, i, -1) for h in range(2)]
    return units


def split_order():
    units = [u for steps in FIRST_PASS for name, u in steps if name in ("below", "own", "second")]
    for i in SECOND:
        units += [(i, c, h) for c in range(LAST, i, -1) for h in range(2) if (i, c, h) not in units]
    return units


RING0 = ring_order()
SPLIT0 = split_order()
PASS1_RING = 2 * (6 * (SLABS - 1) + LAST)
PASS1_SPLIT = sum(name in ("below", "own", "second") for steps in FIRST_PASS for name, _ in steps)
EVACS0 = 2 * SLABS - 1

ABOVE = [u for u in RING0[:PASS1_RING] if u[1] > u[0]]

AT = dict(turn_o=1, x=5, stats=7, h=10, turn_h=10, hT=13, times_w=12, s_next=15)
AT_FIRST = dict(turn_o=1, x=4, stats=5, h=8, turn_h=7, hT=10, times_w=9, s_next=12)
AT_HYP = dict(turn_o=1, relu=5, squares=7, post=9, tanh=12, x=12, stats=13, h=17, turn_h=16, hT=20, times_w=19, s_next=25)
AT_HYP0 = dict(turn_o=1, relu=4, squares=4, post=6, tanh=8, x=8, stats=8, h=10, turn_h=9, hT=11, times_w=10, s_next=13)

GROUPS = [(6, 2), (4, 2), (2, 2), (0, 2)]
PASS2 = len(SPLIT0) - PASS1_SPLIT
POST0_FROM = [2, 6, 11, 15, 20, 27, 38, PASS2]
POST0 = dict(turn_o=0, x=4, stats=5, h=9, turn_h=8, hT=12, times_w=11, s_next=15)
POST0_LAST = dict(turn_o=1, x=3, stats=3, h=5, turn_h=4, hT=6, times_w=5, s_next=7)
HYP_FROM = [21, 34, 47, PASS2 + 7]
HYP = dict(hyp1=-3, hyp2=-1, logs=2, hypm=0, hyp3=3, tanh=6, hyp4=6, logs_sum=8, hyp5=8, times_m=10, hyp6=10)
HYP_LAST = dict(hyp1=-2, hyp2=-1, logs=0, hypm=0, hyp3=1, tanh=1, hyp4=1, logs_sum=2, hyp5=2, times_m=3, hyp6=3)


def schedule():
    at = {}
    for n, base in enumerate(POST0_FROM):
        for name, off in (POST0 if n < SLABS - 1 else POST0_LAST).items():
            at.setdefault(base + off, []).append((name, n))
    for q, base in enumerate(HYP_FROM):
        for name, off in (HYP if q < len(GROUPS) - 1 else HYP_LAST).items():
            at.setdefault(base + off, []).append((name, q))
    return at


SCHEDULE = schedule()


def split_index(layer, slab, u):
    return layer * SLABS * UNITS_PER_SLAB + slab * UNITS_PER_SLAB + u


def ring_laps(layer, slab):
    return len(RING0) // RING + (layer - 1) * SLABS * RING_PER_SLAB // RING + slab * (RING_PER_SLAB // RING)


def evac_index(layer, slab):
    return EVACS0 + (layer - 1) * SLABS + slab


def slab0_chunks(layer):
    return list(range(LAST, -1, -1)) if layer == 1 else list(range(CHUNKS))


def place(layer, slab):
    return LAST - slab if layer == 1 else slab


def build(nc, adj, adj_rows, x_in, w_in, bias_in, out):
    ctx = ExitStack()
    with ctx:
        def sb(name, shape, dt=FP32):
            return ctx.enter_context(nc.sbuf_tensor(name, shape, dt))

        def pb(name, shape):
            return ctx.enter_context(nc.psum_tensor(name, shape, FP32))

        def sem(name):
            return ctx.enter_context(nc.semaphore(name))

        raw = sb("raw", [P, RING, UNIT])
        res = sb("res", [P, SLABS, 2 * UNIT])
        diag0 = sb("diag0", [P, 2 * UNIT])
        diag1 = sb("diag1", [P, 2 * UNIT])
        diag = [diag0, diag1]
        scaled = diag0[:, 0:SLAB].rearrange("p (t f) -> p t f", f=F)
        hi = sb("hi", [P, SPLIT, UNIT], FP32R)
        lo = sb("lo", [P, SPLIT, UNIT], FP32R)
        x = sb("x", [P, N // P, F])
        s_next = sb("s_next", [P, N // P, F])
        s_hi = sb("s_hi", [P, N // P, F], FP32R)
        s_lo = sb("s_lo", [P, N // P, F], FP32R)
        w = sb("w", [P, LAYERS, F])
        bias = sb("bias", [P, 3, F])
        hyp_b = sb("hyp_b", [P, 1, F])
        o_sb = sb("o_sb", [P, SLAB])
        h = sb("h", [P, TILES, F])
        hT = sb("hT", [P, SLAB])
        above = sb("above", [P, 2, TILES, CHUNKS])
        above_sum = sb("above_sum", [P, TILES])
        row_part = o_sb
        ident = sb("ident", [P, P])
        ident_r = sb("ident_r", [P, P], FP32R)
        ones = sb("ones", [P, P])
        mean_r = sb("mean_r", [P, P], FP32R)
        scale_d = sb("scale_d", [P, N // P])
        deg1 = sb("deg1", [P, TILES])
        minus_half = sb("minus_half", [P, TILES])
        half = sb("half", [P, 2, 2 * TILES])
        stats = sb("stats", [P, TILES, 6])
        mv = sb("mv", [P, TILES, 2])
        var_eps = sb("var_eps", [P, TILES])
        minus_mean = sb("minus_mean", [P, TILES])
        above_zero = sb("above_zero", [P, 2, TILES])
        rstd = sb("rstd", [P, TILES])
        ln_scale = sb("ln_scale", [P, TILES])
        ln_bias = sb("ln_bias", [P, TILES])
        spare = sb("spare", [P, 1])
        junk_a = diag1[:, 0:UNIT].rearrange("p (t f) -> p t f", f=F)
        junk_v = diag1[:, UNIT:2 * UNIT].rearrange("p (t f) -> p t f", f=F)
        sq = sb("sq", [P, 2, 2, 2 * TILES])
        nrm = sb("nrm", [P, 2, 2 * TILES])
        hyp = sb("hyp", [P, 32, 2 * TILES])
        bstat = sb("bstat", [P, 16])
        w_b = sb("w_b", [P, 1])

        acc = [pb(f"acc{b}", [P, SLAB]) for b in range(2)]
        row_ps = [pb(f"row_ps{b}", [P, SLAB]) for b in range(2)]
        dot_ps = row_ps
        deg_ps = pb("deg_ps", [P, TILES])
        o_ps = pb("o_ps", [P, TILES, P])
        h_ps = pb("h_ps", [P, SLAB])
        m_ps = pb("m_ps", [P, TILES, F])

        raw_landed = [sem(f"raw_landed{n}") for n in range(RING)]
        res_landed = sem("res_landed")
        diag_landed = sem("diag_landed")
        consts_landed = sem("consts_landed")
        out_landed = sem("out_landed")
        pool_consts = sem("pool_consts")
        act_consts = sem("act_consts")
        dve_consts = sem("dve_consts")
        hi_ready = sem("hi_ready")
        lo_ready = sem("lo_ready")
        unit_used = sem("unit_used")
        s_hi_ready = sem("s_hi_ready")
        s_lo_ready = sem("s_lo_ready")
        acc_free = sem("acc_free")
        row_step = sem("row_step")
        above_ready = sem("above_ready")
        above_summed = sem("above_summed")
        rows_summed = sem("rows_summed")
        deg_ready = sem("deg_ready")
        deg1_ready = sem("deg1_ready")
        d_ready = sem("d_ready")
        o_turned = sem("o_turned")
        relu_ready = sem("relu_ready")
        post_step = [sem(f"post_step{n}") for n in range(LAYERS)]
        post_raised = sem("post_raised")
        post_tanh = sem("post_tanh")
        x_ready = sem("x_ready")
        stats_ready = sem("stats_ready")
        mv_ready = sem("mv_ready")
        var_ready = sem("var_ready")
        rstd_ready = sem("rstd_ready")
        scale_ready = sem("scale_ready")
        ln_ready = sem("ln_ready")
        h_ready = sem("h_ready")
        h_turned = sem("h_turned")
        hT_ready = sem("hT_ready")
        m_ready = sem("m_ready")
        h_squared = sem("h_squared")
        m_squared = sem("m_squared")
        hyp_step = sem("hyp_step")
        hyp_to_pool = sem("hyp_to_pool")
        hyp_pow = sem("hyp_pow")
        hyp_to_act = sem("hyp_to_act")
        hyp_act = sem("hyp_act")
        m_copied = sem("m_copied")
        hyp_done = sem("hyp_done")
        wb_ready = sem("wb_ready")
        bias_step = sem("bias_step")
        bias_pow = sem("bias_pow")
        bias_tanh = sem("bias_tanh")

        HYP_TO_ACT = 3 * len(GROUPS)
        HYP_TO_POOL = 3 * len(GROUPS)
        LINKS = {0: 1, 1: 7, 2: 1, 3: 0}

        def rows(t, slab, k=None):
            return t[:, bass.ds(slab * TILES, TILES), :] if k is None else t[:, bass.ds(slab * TILES + k, 1), :]

        def d_of(slab, k=None):
            return scale_d[:, bass.ds(slab * TILES, TILES)] if k is None else scale_d[:, bass.ds(slab * TILES + k, 1)]

        def source0(unit):
            i, c, hh = unit
            if c == LAST:
                return res[:, i, hh * UNIT:(hh + 1) * UNIT], res_landed, 16 * (i + 1)
            if c == i:
                return diag[i % 2][:, hh * UNIT:(hh + 1) * UNIT], diag_landed, 16 * (i + 1)
            n = RING0.index(unit) if c < i else len(RING0) - 1 - RING0[::-1].index(unit)
            return raw[:, n % RING, :], raw_landed[n % RING], 16 * (n // RING + 1)

        def source(layer, slab, u, chunks):
            c, hh = chunks[u // 2], u % 2
            if c == LAST:
                return res[:, bass.ds(slab, 1), hh * UNIT:(hh + 1) * UNIT], None, None
            r = u - (2 if LAST in chunks[:u // 2] else 0)
            return raw[:, r % RING:r % RING + 1, :], raw_landed[r % RING], (ring_laps(layer, slab) + r // RING + 1) * 16

        def slabs_of(eng, layer, body):
            body(layer, 0, slab0_chunks(layer))
            body(layer, 1, list(range(CHUNKS)))
            with eng.Fori(0, (SLABS - 2) // 2) as it:
                body(layer, it * 2 + 2, list(range(CHUNKS)), 0)
                body(layer, it * 2 + 3, list(range(CHUNKS)), 1)

        def steps_after(after, layer, slab, u):
            n = layer * SLABS + slab - 1
            if isinstance(slab, int) and slab == 0:
                if layer == 2:
                    after(n - 1, LAST - 1, u + UNITS_PER_SLAB, AT_HYP, layer)
                after(n, LAST, u, AT_HYP0 if layer == 2 else AT_FIRST, layer)
            else:
                if layer == 1 and not (isinstance(slab, int) and slab == 1):
                    after(n - 1, slab - 2, u + UNITS_PER_SLAB, AT_HYP, layer + 1)
                after(n, slab - 1, u, AT_HYP if layer == 1 else AT, layer + 1)

        block = ctx.enter_context(nc.Block())

        @block.sync
        def _(sp):
            def load_unit(slot, row, user, used, landed, adj=adj):
                if user is not None:
                    sp.wait_ge(user, used)
                sp.dma_start(raw[:, slot, :], adj[bass.ds(row, P), :]).then_inc(landed, 16)

            def row_of(i, c, hh):
                return ((i * CHUNKS + c) * 2 + hh) * P

            def user_of(n):
                if n < PASS1_RING and RING0[n] in ABOVE:
                    return above_ready, ABOVE.index(RING0[n]) + 1
                return lo_ready, SPLIT0.index(RING0[n]) + 1

            def load0(n):
                user, used = user_of(n - RING) if n >= RING else (None, None)
                above = n < PASS1_RING and RING0[n] in ABOVE
                load_unit(n % RING, row_of(*RING0[n]), user, used, raw_landed[n % RING], adj_rows if above else adj)

            sp.dma_start(x[:], x_in).then_inc(consts_landed, 16)
            sp.dma_start(w[:], w_in).then_inc(consts_landed, 16)
            sp.dma_start(bias[:], bias_in).then_inc(consts_landed, 16)
            for i in range(SLABS):
                ns = [n for n in range(PASS1_RING) if RING0[n][0] == i]
                for k, n in enumerate(ns):
                    if k == RING:
                        both = adj[row_of(i, LAST, 0):row_of(i, LAST, 0) + 2 * P, :].rearrange("(h p) n -> p h n", p=P)
                        sp.dma_start(res[:, i, :].rearrange("p (h n) -> p h n", h=2), both).then_inc(res_landed, 16)
                        if i < LAST:
                            if i == 1:
                                sp.wait_ge(bias_step, 8)
                            if i >= 2:
                                sp.wait_ge(lo_ready, SPLIT0.index((i - 2, i - 2, 1)) + 1)
                            both = adj[row_of(i, i, 0):row_of(i, i, 0) + 2 * P, :].rearrange("(h p) n -> p h n", p=P)
                            sp.dma_start(diag[i % 2][:].rearrange("p (h n) -> p h n", h=2), both).then_inc(diag_landed, 16)
                    load0(n)
            for n in range(PASS1_RING, len(RING0)):
                load0(n)

            def body(layer, slab, chunks, parity=None):
                skip = 2 if layer == 1 and isinstance(slab, int) else 0
                first = isinstance(slab, int) and slab == 0
                for r, (c, hh) in enumerate((c, hh) for c in chunks if c != LAST for hh in range(2)):
                    if r >= RING:
                        u = r - RING + (skip if first else 0)
                        user, used = lo_ready, split_index(layer, slab, u) + 1
                    elif first and layer == 1:
                        user, used = user_of(len(RING0) - RING + r)
                    else:
                        user, used = lo_ready, split_index(layer, slab, r + RING + skip) - UNITS_PER_SLAB + 1
                    load_unit(r % RING, slab * (CHUNKS * 2 * P) + (c * 2 + hh) * P, user, used, raw_landed[r % RING])

            for layer in range(1, LAYERS):
                slabs_of(sp, layer, body)

        @block.scalar
        def _(act):
            def split_hi(src, landed, value, g, slot):
                if landed is not None:
                    act.wait_ge(landed, value)
                if not isinstance(g, int) or g >= SPLIT:
                    act.wait_ge(unit_used, g - SPLIT + 1)
                nc.scalar.copy(hi[:, slot:slot + 1, :] if len(src.shape) == 3 else hi[:, slot, :], src).then_inc(hi_ready, 1)

            def free_acc(units, bank, dst):
                act.wait_ge(unit_used, units)
                nc.scalar.copy(dst, acc[bank][:]).then_inc(acc_free, 1)

            def squares(src, kind, at, group=0):
                for k in range(TILES):
                    last = nc.scalar.activation(junk_a[:, kind * TILES + k, :], src[:, k:k + 1, :], ACT.Square,
                                                accum_out=sq[:, group, kind, at + k:at + k + 1])
                return last

            def h_step(p, slab):
                act.wait_ge(ln_ready, p + 1)
                if not isinstance(p, int) or p >= 1:
                    act.wait_ge(h_turned, p)
                for k in range(TILES):
                    last = nc.scalar.activation(h[:, k:k + 1, :], rows(x, slab, k), ACT.Relu,
                                                bias=ln_bias[:, k:k + 1], scale=ln_scale[:, k:k + 1])
                last.then_inc(h_ready, 1)

            def hT_step(p):
                act.wait_ge(h_turned, p + 1)
                if not isinstance(p, int) or p >= 1:
                    act.wait_ge(m_ready, p)
                nc.scalar.copy(hT[:], h_ps[:]).then_inc(hT_ready, 1)

            def s_next_step(p, slab, seen):
                act.wait_ge(m_ready, p + 1)
                if seen is not None:
                    act.wait_ge(s_lo_ready, seen)
                nc.scalar.copy(rows(s_next, slab), m_ps[:]).then_inc(m_copied, 1)

            def split_s(layer, slab):
                m = layer * SLABS + place(layer, slab)
                if layer == 1:
                    act.wait_ge(hyp_done, place(layer, slab) + 1)
                else:
                    act.wait_ge(m_copied, m + 1)
                nc.scalar.copy(rows(s_hi, slab), rows(s_next, slab)).then_inc(s_hi_ready, 1)

            def after(n, slab, at, table, layer):
                p = n + SLABS
                if at == table.get("relu"):
                    q = n - SLABS
                    act.wait_ge(o_turned, n + 1)
                    act.wait_ge(h_turned, p)
                    act.wait_ge(hyp_pow, HYP_TO_POOL + q)
                    nc.scalar.activation(h[:], o_ps[:], ACT.Relu).then_inc(relu_ready, 1)
                    squares(o_ps, 0, 0)
                if at == table.get("squares"):
                    q = n - SLABS
                    act.wait_ge(relu_ready, 2 * q + 1)
                    squares(h, 1, 0).then_inc(relu_ready, 1)
                if at == table.get("tanh"):
                    act.wait_ge(hyp_to_act, HYP_TO_ACT + n - SLABS + 1)
                    nc.scalar.activation(hyp[:, 2, 0:TILES], hyp[:, 1, 0:TILES], ACT.Tanh).then_inc(post_tanh, 1)
                if at == table["h"]:
                    h_step(p, slab)
                if at == table["hT"]:
                    hT_step(p)
                if at == table["s_next"]:
                    s_next_step(p, slab, layer * SLABS)

            def scheduled(t):
                for name, n in SCHEDULE.get(t, []):
                    if name in POST0:
                        p, slab = n + SLABS, LAST - n
                        half_at = next(slab - s0 for s0, width in GROUPS if s0 <= slab < s0 + width) * TILES
                        q = next(q for q, (s0, width) in enumerate(GROUPS) if s0 <= slab < s0 + width)
                    else:
                        q = n
                        w4 = GROUPS[q][1] * TILES
                        V = lambda i: hyp[:, i, 0:w4]
                    if name == "h":
                        if n >= 1:
                            act.wait_ge(h_squared, n)
                        h_step(p, slab)
                        if q >= 2:
                            act.wait_ge(hyp_to_pool, 3 * q - 4)
                        act.wait_ge(h_ready, p + 1)
                        squares(h, 0, half_at, q % 2).then_inc(h_squared, 1)
                    if name == "hT":
                        hT_step(p)
                    if name == "s_next":
                        s_next_step(p, slab, SLABS)
                        act.wait_ge(m_copied, p + 1)
                        squares(rows(s_next, slab), 1, half_at, q % 2).then_inc(m_squared, 1)
                    if name == "logs":
                        act.wait_ge(hyp_to_act, 3 * q + 1)
                        nc.scalar.activation(V(1), V(0), ACT.Ln, bias=1.0)
                        nc.scalar.activation(V(2), V(0), ACT.Ln, bias=1.0, scale=-1.0).then_inc(hyp_act, 1)
                    if name == "tanh":
                        act.wait_ge(hyp_to_act, 3 * q + 2)
                        nc.scalar.activation(V(8), V(7), ACT.Tanh).then_inc(hyp_act, 1)
                    if name == "logs_sum":
                        act.wait_ge(hyp_pow, 3 * q + 3)
                        nc.scalar.activation(V(20), V(18), ACT.Ln, bias=1.0)
                        nc.scalar.activation(V(21), V(16), ACT.Ln).then_inc(hyp_act, 1)
                    if name == "times_m":
                        act.wait_ge(hyp_to_act, 3 * q + 3)
                        for k in range(w4):
                            sk = rows(s_next, GROUPS[q][0], k)
                            last = nc.scalar.activation(sk, sk, ACT.Copy, scale=hyp[:, 24, k:k + 1])
                        last.then_inc(hyp_act, 1)

            act.wait_ge(pool_consts, 2)
            nc.scalar.copy(ident_r[:], ident[:])
            nc.scalar.mul(mean_r[:], ones[:], 1.0 / P).then_inc(act_consts, 1)
            act.wait_ge(consts_landed, 48)
            nc.scalar.activation(junk_a[:, 0, :], bias[:, 1, :], ACT.Square, accum_out=bstat[:, 0:1]).then_inc(bias_step, 1)
            act.wait_ge(bias_step, 3)
            nc.scalar.activation(bstat[:, 4:5], bstat[:, 3:4], ACT.Tanh).then_inc(bias_tanh, 1)

            def split0(g):
                src, landed, value = source0(SPLIT0[g])
                split_hi(src, landed, value, g, g % SPLIT)

            h_step(0, 0)
            hT_step(0)
            s_next_step(0, 0, None)
            for i in range(SLABS + 1):
                for name, unit in FIRST_PASS[i]:
                    if name in ("below", "own", "second"):
                        split0(SPLIT0.index(unit))
                    if name == "above":
                        _, c, hh = unit
                        n = RING0.index(unit)
                        act.wait_ge(raw_landed[n % RING], 16 * (n // RING + 1))
                        for e in range(2):
                            half_unit = raw[:, n % RING, e * SLAB:(e + 1) * SLAB]
                            last = nc.scalar.activation(half_unit, half_unit, ACT.Copy,
                                                        accum_out=above[:, i % 2, 2 * hh + e, c:c + 1])
                        last.then_inc(above_ready, 1)
                    if name == "scale":
                        act.wait_ge(m_copied, i)
                        act.wait_ge(d_ready, i)
                        for k in range(TILES):
                            last = nc.scalar.activation(rows(s_hi, i - 1, k), rows(s_next, i - 1, k), ACT.Copy,
                                                        scale=d_of(i - 1, k))
                        last.then_inc(s_hi_ready, 1)
                    if name == "evac" and i < SLABS:
                        act.wait_ge(s_lo_ready, i)
                        free_acc(SPLIT0.index((i - 1, i - 1, 1)) + 1, (i - 1) % 2,
                                 rows(s_next, i - 1).rearrange("p t f -> p (t f)"))
                    if name == "h":
                        h_step(i + 1, i + 1)
                    if name == "hT":
                        hT_step(i + 1)
                    if name == "s_next":
                        s_next_step(i + 1, i + 1, None)

            for u in range(PASS2):
                split0(PASS1_SPLIT + u)
                if u == 1:
                    act.wait_ge(s_lo_ready, SLABS)
                    free_acc(PASS1_SPLIT, LAST % 2, rows(s_next, LAST).rearrange("p t f -> p (t f)"))
                scheduled(u)

            def body(layer, slab, chunks, parity=None):
                first = isinstance(slab, int) and slab == 0
                if isinstance(slab, int):
                    parity = slab % 2
                n = layer * SLABS + slab - 1
                prev, lay = (LAST, layer) if first else (slab - 1, layer + 1)
                for u in range(UNITS_PER_SLAB):
                    if first and u % 2 == 0:
                        split_s(layer, chunks[u // 2])
                    src, landed, value = source(layer, slab, u, chunks)
                    split_hi(src, landed, value, split_index(layer, slab, u), u % SPLIT)
                    if first and layer == 1:
                        scheduled(PASS2 + u)
                        continue
                    if u == 3:
                        act.wait_ge(o_turned, n)
                        free_acc(split_index(layer, slab, 0), parity, o_sb[:])
                    if lay < LAYERS:
                        steps_after(after, layer, slab, u)
                    elif u == AT["h"]:
                        send(n, prev)

            def send(n, slab):
                act.wait_ge(x_ready, n + 1)
                act.dma_start(out[:, bass.ds(slab * TILES, TILES), :], rows(x, slab)).then_inc(out_landed, 16)

            for layer in range(1, LAYERS):
                slabs_of(act, layer, body)
            n = LAYERS * SLABS - 1
            act.wait_ge(o_turned, n)
            free_acc(split_index(LAYERS, 0, 0), (evac_index(LAYERS, 0) - 1) % 2, o_sb[:])
            send(n, LAST)
            act.wait_ge(out_landed, 16 * SLABS)

        @block.vector
        def _(dve):
            steps = {}

            def link(s, ins, base=0):
                steps[s.name] = steps.get(s.name, 0) + 1
                ins.then_inc(s, 1)
                dve.wait_ge(s, base + steps[s.name])

            def split_lo(src, g, slot):
                dve.wait_ge(hi_ready, g + 1)
                flat = len(src.shape) == 2
                hs = hi[:, slot, :] if flat else hi[:, slot:slot + 1, :]
                ls = lo[:, slot, :] if flat else lo[:, slot:slot + 1, :]
                last = nc.vector.tensor_tensor(ls, src, hs.bitcast(FP32), ALU.subtract)
                last.then_inc(lo_ready, 1)
                return last

            def x_step(n, slab, layer):
                src = layer - 1
                base = (n - src * SLABS) * LINKS[src]
                if src != 1:
                    steps[post_step[src].name] = 0
                dve.wait_ge(o_turned, n + 1)
                xs = rows(x, slab)
                if src in (0, 2):
                    for k in range(TILES):
                        last = nc.vector.scalar_tensor_tensor(scaled[:, k:k + 1, :], o_ps[:, k:k + 1, :], d_of(slab, k),
                                                              bias[:, src:src + 1, :], ALU.mult, ALU.add)
                    link(post_step[src], last, base)
                    if src == 0:
                        last = nc.vector.scalar_tensor_tensor(xs, scaled, 0.0, xs, ALU.max, ALU.add)
                    else:
                        last = nc.vector.tensor_tensor(xs, scaled, xs, ALU.add)
                if src == 3:
                    last = nc.vector.scalar_tensor_tensor(xs, o_ps[:], 0.0, xs, ALU.max, ALU.add)
                if src == 1:
                    q = n - SLABS
                    st = post_step[1]
                    g, vn, rv, out_scale = (hyp[:, r, 0:TILES] for r in (6, 1, 8, 11))
                    dve.wait_ge(post_tanh, q + 1)
                    steps[st.name] = 5
                    link(st, nc.vector.scalar_tensor_tensor(hyp[:, 9, 0:TILES], hyp[:, 2, 0:TILES], MAXNORM, rv,
                                                            ALU.min, ALU.mult), base)
                    link(st, nc.vector.tensor_tensor(out_scale, hyp[:, 9, 0:TILES], g, ALU.mult), base)
                    for k in range(TILES):
                        xk = rows(x, slab, k)
                        last = nc.vector.scalar_tensor_tensor(xk, h[:, k:k + 1, :], hyp[:, 11, k:k + 1], xk,
                                                              ALU.mult, ALU.add)
                last.then_inc(x_ready, 1)
                assert steps[post_step[src].name] == LINKS[src], steps

            def carry_wait():
                nc.vector.memset(spare[:], 0.0)

            def post_step_of(n):
                q, st = n - SLABS, post_step[1]
                base = q * LINKS[1]
                steps[st.name] = 0
                un, rn = nrm[:, 0, 0:TILES], nrm[:, 1, 0:TILES]
                iu, g, v, vn, rv = (hyp[:, r, 0:TILES] for r in (4, 6, 7, 1, 8))
                dve.wait_ge(hyp_pow, HYP_TO_POOL + q + 1)
                link(st, nc.vector.tensor_scalar(nrm[:, :, 0:TILES], nrm[:, :, 0:TILES], TINY, None, ALU.max), base)
                link(st, nc.vector.reciprocal(iu, un), base)
                link(st, nc.vector.scalar_tensor_tensor(g, un, ATANH_MAX, iu, ALU.min, ALU.mult), base)
                link(st, nc.vector.tensor_tensor(v, g, rn, ALU.mult), base)
                nc.vector.tensor_scalar(vn, v, TINY, None, ALU.max).then_inc(hyp_to_act, 1)
                dve.wait_ge(hyp_to_act, HYP_TO_ACT + q + 1)
                link(st, nc.vector.reciprocal(rv, vn), base)

            def stats_step(p, slab, xr):
                if xr is not None:
                    dve.wait_ge(x_ready, xr)
                    carry_wait()
                for k in range(TILES):
                    last = nc.vector.bn_stats(stats[:, k, :], rows(x, slab, k))
                last.then_inc(stats_ready, 1)
                dve.wait_ge(stats_ready, p + 1)
                carry_wait()
                for k in range(TILES):
                    last = nc.vector.bn_aggr(mv[:, k, :], stats[:, k, :])
                last.then_inc(mv_ready, 1)
                dve.wait_ge(mv_ready, p + 1)
                if not isinstance(p, int) or p >= 1:
                    dve.wait_ge(ln_ready, p)
                nc.vector.tensor_scalar(var_eps[:], mv[:, :, 1], LN_EPS, None, ALU.add)
                nc.vector.tensor_scalar(minus_mean[:], mv[:, :, 0], -1.0, None, ALU.mult).then_inc(var_ready, 1)

            done = {"steps": 0, "seen": 0}

            def do(ins):
                ins.then_inc(hyp_step, 1)
                done["steps"] += 1
                return done["steps"]

            def needs(step):
                if step > done["seen"]:
                    dve.wait_ge(hyp_step, step)
                    done["seen"] = step

            def tt(o, a, b, op, need=0):
                needs(need)
                return do(nc.vector.tensor_tensor(o, a, b, op))

            def ts(o, a, s1, op0, need=0, s2=None, op1=None):
                needs(need)
                return do(nc.vector.tensor_scalar(o, a, s1, s2, op0, *([] if op1 is None else [op1])))

            def stt(o, a, s, b, op0, op1, need=0):
                needs(need)
                return do(nc.vector.scalar_tensor_tensor(o, a, s, b, op0, op1))

            def hyper(q, step):
                slab, width = GROUPS[q]
                w4 = width * TILES
                V = lambda i: hyp[:, i, 0:w4]
                h_norm, m_norm = nrm[:, 0, 0:w4], nrm[:, 1, 0:w4]
                if step == "1":
                    dve.wait_ge(h_squared, LAST - slab + 1)
                    nc.vector.tensor_scalar(V(4), sq[:, q % 2, 0, 0:w4], TINY2, None, ALU.max).then_inc(hyp_to_pool, 1)
                    dve.wait_ge(hyp_to_pool, 3 * q + 1)
                if step == "m":
                    dve.wait_ge(m_squared, LAST - slab + 1)
                    do(nc.vector.tensor_copy(V(3), dot_ps[q % 2][:, 0:w4]))
                    nc.vector.tensor_scalar(V(5), sq[:, q % 2, 1, 0:w4], TINY2, None, ALU.max).then_inc(hyp_to_pool, 1)
                if step == "2":
                    dve.wait_ge(hyp_pow, 3 * q + 1)
                    nc.vector.tensor_scalar(V(0), h_norm, CLIP, None, ALU.min).then_inc(hyp_to_act, 1)
                    a = ts(V(12), V(4), SERIES[0], ALU.mult)
                    do(nc.vector.reciprocal(V(9), h_norm))
                    for coef in SERIES[1:]:
                        a = stt(V(12), V(12), coef, V(4), ALU.add, ALU.mult, need=a)
                    ts(V(11), V(12), 1.0, ALU.add, need=a)
                if step == "3":
                    needs(done["steps"])
                    dve.wait_ge(hyp_act, 4 * q + 1)
                    a = tt(V(13), V(1), V(2), ALU.subtract)
                    a = stt(V(14), V(13), 0.5, V(9), ALU.mult, ALU.mult, need=a)
                    a = tt(V(12), V(11), V(14), ALU.subtract, need=a)
                    a = stt(V(12), h_norm, SERIES_BELOW, V(12), ALU.is_lt, ALU.mult, need=a)
                    a = tt(V(13), V(12), V(14), ALU.add, need=a)
                    needs(a)
                    dve.wait_ge(hyp_pow, 3 * q + 2)
                    nc.vector.tensor_tensor(V(7), V(13), m_norm, ALU.mult).then_inc(hyp_to_act, 1)
                    do(nc.vector.reciprocal(V(10), m_norm))
                if step == "4":
                    y2, one_y2 = bstat[:, 8:9], bstat[:, 9:10]
                    needs(done["steps"])
                    dve.wait_ge(hyp_act, 4 * q + 2)
                    a = stt(V(11), V(8), MAXNORM, V(10), ALU.min, ALU.mult)
                    b = tt(V(13), V(11), V(3), ALU.mult, need=a)
                    a = tt(V(12), V(11), V(11), ALU.mult)
                    b = ts(V(14), V(13), 2.0, ALU.mult, b, 1.0, ALU.add)
                    a = tt(V(15), V(12), V(5), ALU.mult, need=a)
                    b = stt(V(19), V(14), y2, V(11), ALU.add, ALU.mult, need=b)
                    c = stt(V(13), V(15), y2, V(14), ALU.mult, ALU.add, need=a)
                    a = ts(V(12), V(15), -1.0, ALU.mult, a, 1.0, ALU.add)
                    c = ts(V(22), V(13), TINY, ALU.max, need=c)
                    needs(c)
                    c = do(nc.vector.reciprocal(V(23), V(22)))
                    a = tt(V(14), V(19), V(23), ALU.mult, need=c)
                    b = tt(V(15), V(12), V(23), ALU.mult)
                    stt(V(16), V(12), one_y2, V(23), ALU.mult, ALU.mult)
                    c = tt(V(13), V(14), V(3), ALU.mult, need=a)
                    b = ts(V(19), V(15), y2, ALU.mult, need=b)
                    a = tt(V(22), V(14), V(14), ALU.mult)
                    b = stt(V(27), V(13), 2.0, V(19), ALU.mult, ALU.add, need=b)
                    a = tt(V(28), V(22), V(5), ALU.mult, need=a)
                    b = tt(V(29), V(27), V(15), ALU.mult, need=b)
                    a = tt(V(30), V(29), V(28), ALU.add, need=b)
                    needs(a)
                    nc.vector.tensor_scalar(V(17), V(30), TINY2, None, ALU.max).then_inc(hyp_to_pool, 1)
                    dve.wait_ge(hyp_to_pool, 3 * q + 3)
                    a = ts(V(12), V(17), SERIES[0], ALU.mult)
                    for coef in SERIES[1:]:
                        a = stt(V(12), V(12), coef, V(17), ALU.add, ALU.mult, need=a)
                    ts(V(11), V(12), 1.0, ALU.add, need=a)
                if step == "5":
                    needs(done["steps"])
                    dve.wait_ge(hyp_pow, 3 * q + 3)
                    c = do(nc.vector.reciprocal(V(19), V(18)))
                    dve.wait_ge(hyp_act, 4 * q + 3)
                    a = stt(V(22), V(21), -0.5, V(20), ALU.mult, ALU.add)
                    a = stt(V(23), V(22), ATANH_MAX, V(19), ALU.min, ALU.mult, need=a)
                    b = tt(V(12), V(11), V(23), ALU.subtract, need=a)
                    b = stt(V(13), V(18), SERIES_BELOW, V(12), ALU.is_lt, ALU.mult, need=b)
                    b = tt(V(22), V(13), V(23), ALU.add, need=b)
                    tt(V(25), V(22), V(15), ALU.mult, need=b)
                    nc.vector.tensor_tensor(V(24), V(22), V(14), ALU.mult).then_inc(hyp_to_act, 1)
                if step == "6":
                    needs(done["steps"])
                    dve.wait_ge(hyp_act, 4 * q + 4)
                    for k in [j * TILES + t for j in reversed(range(width)) for t in range(TILES)]:
                        sk = rows(s_next, slab, k)
                        last = nc.vector.scalar_tensor_tensor(sk, hyp_b[:], hyp[:, 25, k:k + 1], sk, ALU.mult, ALU.add)
                        if k % TILES == TILES - 1:
                            last.then_inc(hyp_done, 1)

            def scheduled(t):
                for name, n in SCHEDULE.get(t, []):
                    if name == "x":
                        x_step(n, LAST - n, 1)
                    if name == "stats":
                        stats_step(n + SLABS, LAST - n, n + 1)
                    if name[:3] == "hyp":
                        hyper(n, name[3])

            def after(n, slab, at, table, layer):
                p = n + SLABS
                if at == table.get("post"):
                    post_step_of(n)
                if at == table["x"]:
                    x_step(n, slab, layer)
                if layer < LAYERS and at == table["stats"]:
                    stats_step(p, slab, n + 1)

            def split_s(layer, slab):
                m = layer * SLABS + place(layer, slab)
                dve.wait_ge(s_hi_ready, m + 1)
                nc.vector.tensor_tensor(rows(s_lo, slab), rows(s_next, slab), rows(s_hi, slab).bitcast(FP32),
                                        ALU.subtract).then_inc(s_lo_ready, 1)

            nc.vector.memset(half[:], 0.5)
            nc.vector.memset(above_zero[:], ABOVE_ZERO)
            nc.vector.memset(minus_half[:], -0.5).then_inc(dve_consts, 1)
            dve.wait_ge(bias_step, 1)
            nc.vector.tensor_scalar(bstat[:, 1:2], bstat[:, 0:1], TINY2, None, ALU.max).then_inc(bias_step, 1)
            dve.wait_ge(bias_pow, 1)
            nc.vector.tensor_scalar(bstat[:, 3:4], bstat[:, 2:3], 1.0, None, ALU.mult).then_inc(bias_step, 1)
            dve.wait_ge(bias_step, 3)
            nc.vector.reciprocal(bstat[:, 5:6], bstat[:, 3:4]).then_inc(bias_step, 1)
            dve.wait_ge(bias_tanh, 1)
            nc.vector.tensor_scalar(bstat[:, 6:7], bstat[:, 4:5], MAXNORM, None, ALU.min).then_inc(bias_step, 1)
            dve.wait_ge(bias_step, 5)
            nc.vector.tensor_tensor(bstat[:, 7:8], bstat[:, 6:7], bstat[:, 5:6], ALU.mult).then_inc(bias_step, 1)
            dve.wait_ge(bias_step, 6)
            nc.vector.tensor_scalar(hyp_b[:, 0, :], bias[:, 1, :], bstat[:, 7:8], None, ALU.mult).then_inc(bias_step, 1)
            dve.wait_ge(bias_step, 7)
            dve.wait_ge(consts_landed, 48)
            nc.vector.scalar_tensor_tensor(junk_v[:, 0, :], hyp_b[:, 0, :], 1.0, hyp_b[:, 0, :], ALU.mult, ALU.mult,
                                           accum_out=bstat[:, 8:9]).then_inc(bias_step, 1)
            nc.vector.scalar_tensor_tensor(junk_v[:, 1, :], w[:, 1, :], 1.0, hyp_b[:, 0, :], ALU.mult, ALU.mult,
                                           accum_out=w_b[:]).then_inc(wb_ready, 1)
            dve.wait_ge(bias_step, 8)
            nc.vector.tensor_scalar(bstat[:, 9:10], bstat[:, 8:9], -1.0, 1.0, ALU.mult, ALU.add).then_inc(bias_step, 1)
            dve.wait_ge(bias_step, 9)

            dve.wait_ge(consts_landed, 48)
            stats_step(0, 0, None)

            def add_rows(src, landed, value, fresh=False, final=False):
                dve.wait_ge(landed, value)
                a, b = src[:, 0:SLAB], src[:, SLAB:UNIT]
                if fresh:
                    link(row_step, nc.vector.tensor_tensor(row_part[:], a, b, ALU.add))
                    return
                link(row_step, nc.vector.tensor_tensor(row_part[:], row_part[:], a, ALU.add))
                last = nc.vector.tensor_tensor(row_part[:], row_part[:], b, ALU.add)
                if final:
                    last.then_inc(rows_summed, 1)
                else:
                    link(row_step, last)

            def split0(g):
                src, _, _ = source0(SPLIT0[g])
                split_lo(src, g, g % SPLIT)

            for i in range(SLABS + 1):
                for name, unit in FIRST_PASS[i]:
                    if name == "below" and unit in ROWS_BY_VECTOR:
                        add_rows(*source0(unit))
                    if name in ("below", "own", "second"):
                        split0(SPLIT0.index(unit))
                    if name == "stats":
                        stats_step(i + 1, i + 1, None)
                    if name == "scale":
                        dve.wait_ge(s_hi_ready, i)
                        for k in range(TILES):
                            last = nc.vector.scalar_tensor_tensor(
                                rows(s_lo, i - 1, k), rows(s_next, i - 1, k), d_of(i - 1, k),
                                rows(s_hi, i - 1, k).bitcast(FP32), ALU.mult, ALU.subtract)
                        last.then_inc(s_lo_ready, 1)
                    if name == "rows":
                        for hh in range(2):
                            add_rows(res[:, i, hh * UNIT:(hh + 1) * UNIT], res_landed, 16 * (i + 1), fresh=hh == 0)
                    if name == "own_rows":
                        for hh in range(2):
                            add_rows(diag[i % 2][:, hh * UNIT:(hh + 1) * UNIT], diag_landed, 16 * (i + 1),
                                     final=i == 0 and hh == 1)
                    if name == "sum":
                        k = i - 1
                        if k >= 1:
                            below = [SPLIT0.index(u) for n, u in FIRST_PASS[k] if n == "below"]
                            dve.wait_ge(unit_used, max(below) + 1)
                            nc.vector.tensor_tensor(row_part[:], row_part[:], row_ps[k % 2][:],
                                                    ALU.add).then_inc(rows_summed, 1)
                        if k < LAST - 1:
                            dve.wait_ge(above_ready, sum(2 * (LAST - 1 - j) for j in range(k + 1)))
                            nc.vector.tensor_reduce(above_sum[:], above[:, k % 2, :, k + 1:LAST], mybir.AxisListType.X,
                                                    ALU.add).then_inc(above_summed, 1)
                    if name == "deg1":
                        dve.wait_ge(deg_ready, i)
                        if i - 1 < LAST - 1:
                            dve.wait_ge(above_summed, i)
                            nc.vector.scalar_tensor_tensor(deg1[:], deg_ps[:], 1.0, above_sum[:], ALU.add,
                                                           ALU.add).then_inc(deg1_ready, 1)
                        else:
                            nc.vector.tensor_scalar(deg1[:], deg_ps[:], 1.0, None, ALU.add).then_inc(deg1_ready, 1)

            def second_unit(gg):
                split0(gg)
                for e in range(SLABS, EVACS0 - 1):
                    slab = SECOND[e - SLABS]
                    end = 1 + max(k for k, (i, c, _) in enumerate(SPLIT0) if i == slab and c > i)
                    if gg == end + SPLIT - 2:
                        join(e, slab, end)

            def join(e, slab, units):
                dve.wait_ge(unit_used, units)
                dve.wait_ge(acc_free, e)
                part = rows(s_next, slab).rearrange("p t f -> p (t f)")
                nc.vector.tensor_tensor(part, part, acc[e % 2][:], ALU.add).then_inc(acc_free, 1)

            for u in range(PASS2):
                second_unit(PASS1_SPLIT + u)
                scheduled(u)

            def body(layer, slab, chunks, parity=None):
                n = layer * SLABS + slab - 1
                first = isinstance(slab, int) and slab == 0
                prev, lay = (LAST, layer) if first else (slab - 1, layer + 1)
                for u in range(UNITS_PER_SLAB):
                    if first and u % 2 == 0:
                        split_s(layer, chunks[u // 2])
                    src, _, value = source(layer, slab, u, chunks)
                    split_lo(src, split_index(layer, slab, u), u % SPLIT)
                    if first and layer == 1:
                        if u == 2:
                            join(EVACS0 - 1, 0, len(SPLIT0))
                        scheduled(PASS2 + u)
                    else:
                        steps_after(after, layer, slab, u)

            for layer in range(1, LAYERS):
                slabs_of(dve, layer, body)
            after(LAYERS * SLABS - 1, LAST, AT["x"], AT, LAYERS)

        @block.tensor
        def _(pe):
            def contract(bank, c, hh, slot, first, last_unit, g, rows_to=None, rowsum=None):
                pe.wait_ge(lo_ready, g + 1)
                for t in range(2):
                    j = c * TILES + hh * 2 + t
                    a, b = hi[:, slot, t * SLAB:(t + 1) * SLAB], lo[:, slot, t * SLAB:(t + 1) * SLAB]
                    nc.tensor.matmul(acc[bank][:], s_hi[:, j, :], a, start=first and t == 0, stop=False)
                    nc.tensor.matmul(acc[bank][:], s_hi[:, j, :], b, start=False, stop=False)
                    last = nc.tensor.matmul(acc[bank][:], s_lo[:, j, :], a, start=False, stop=last_unit and t == 1)
                if rowsum is not None:
                    for t in range(2):
                        for k, part in enumerate((hi, lo)):
                            last = nc.tensor.matmul(rows_to[:], mean_r[:], part[:, slot, t * SLAB:(t + 1) * SLAB],
                                                    start=rowsum == 0 and t + k == 0, stop=rowsum == 2 and t + k == 2)
                last.then_inc(unit_used, 1)
                return last

            def turn_o(n, slab, own, src):
                pe.wait_ge(x_ready, n) if not isinstance(n, int) or n >= 1 else None
                for k in range(TILES):
                    last = nc.tensor.matmul(o_ps[:, k, :], src(k), ident[:], is_transpose=True, start=k == 0,
                                            stop=(not own) and k == TILES - 1)
                if own:
                    flat = o_ps[:].rearrange("p t f -> p (t f)")
                    nc.tensor.matmul(flat, ident_r[:], rows(s_hi, slab).rearrange("p t f -> p (t f)"), start=False, stop=False)
                    last = nc.tensor.matmul(flat, ident_r[:], rows(s_lo, slab).rearrange("p t f -> p (t f)"), start=False, stop=True)
                last.then_inc(o_turned, 1)

            def turn_h(p):
                pe.wait_ge(h_ready, p + 1)
                if not isinstance(p, int) or p >= 1:
                    pe.wait_ge(hT_ready, p)
                for k in range(TILES):
                    last = nc.tensor.matmul(h_ps[:, k * P:(k + 1) * P], h[:, k, :], ident[:], is_transpose=True,
                                            start=k == 0, stop=k == TILES - 1)
                last.then_inc(h_turned, 1)

            def times_w(p, layer):
                pe.wait_ge(hT_ready, p + 1)
                if not isinstance(p, int) or p >= 1:
                    pe.wait_ge(m_copied, p)
                for k in range(TILES):
                    last = nc.tensor.matmul(m_ps[:, k, :], hT[:, k * P:(k + 1) * P], w[:, layer, :],
                                            start=k == 0, stop=k == TILES - 1)
                last.then_inc(m_ready, 1)

            def after(n, slab, at, table, layer):
                if at == table["turn_o"]:
                    pe.wait_ge(acc_free, EVACS0 - SLABS + n + 1)
                    turn_o(n, slab, layer == 3, lambda k: o_sb[:, k * P:(k + 1) * P])
                if layer < LAYERS and at == table["turn_h"]:
                    turn_h(n + SLABS)
                if layer < LAYERS and at == table["times_w"]:
                    times_w(n + SLABS, layer)

            def scheduled(t):
                for name, n in SCHEDULE.get(t, []):
                    slab = LAST - n
                    if name == "turn_o":
                        pe.wait_ge(acc_free, SLABS if n == 0 else SLABS + SECOND.index(slab) + 1)
                        turn_o(n, slab, True, lambda k: s_next[:, slab * TILES + k, :])
                    if name == "turn_h":
                        turn_h(n + SLABS)
                    if name == "times_w":
                        q = next(q for q, (s0, width) in enumerate(GROUPS) if s0 <= slab < s0 + width)
                        pe.wait_ge(hT_ready, n + SLABS + 1)
                        if q == 0:
                            pe.wait_ge(wb_ready, 1)
                        if q >= 2:
                            pe.wait_ge(hyp_to_pool, 3 * q - 4)
                        at = (slab - GROUPS[q][0]) * TILES
                        for k in range(TILES):
                            nc.tensor.matmul(dot_ps[q % 2][:, at + k:at + k + 1], hT[:, k * P:(k + 1) * P], w_b[:],
                                             start=k == 0, stop=k == TILES - 1)
                        times_w(n + SLABS, 1)

            pe.wait_ge(pool_consts, 2)
            pe.wait_ge(consts_landed, 48)
            turn_h(0)
            times_w(0, 0)
            pe.wait_ge(act_consts, 1)

            def second_unit(gg):
                i, c, hh = SPLIT0[gg]
                e = SLABS + SECOND.index(i)
                mine = [k for k, (j, cc, _) in enumerate(SPLIT0) if j == i and cc > j]
                if gg == mine[0]:
                    pe.wait_ge(acc_free, e - 1)
                contract(e % 2, c, hh, gg % SPLIT, gg == mine[0], gg == mine[-1], gg)

            for i in range(SLABS + 1):
                below = [u for name, u in FIRST_PASS[i] if name == "below"]
                for name, unit in FIRST_PASS[i]:
                    if name == "below":
                        g = SPLIT0.index(unit)
                        if unit == below[0] and i >= 2:
                            pe.wait_ge(acc_free, i - 1)
                            pe.wait_ge(rows_summed, i - 1)
                        summed = [u for u in below if u not in ROWS_BY_VECTOR]
                        rowsum = 1 if unit in summed else None
                        if unit == summed[0]:
                            rowsum = 0
                        if unit == summed[-1]:
                            rowsum = 2
                        contract(i % 2, unit[1], unit[2], g % SPLIT, unit == below[0], False, g, row_ps[i % 2], rowsum)
                    if name == "second":
                        second_unit(SPLIT0.index(unit))
                    if name == "own":
                        g = SPLIT0.index(unit)
                        pe.wait_ge(s_lo_ready, i)
                        contract((i - 1) % 2, i - 1, unit[2], g % SPLIT, i == 1 and unit[2] == 0, unit[2] == 1, g)
                    if name == "turn_h":
                        turn_h(i + 1)
                    if name == "times_w":
                        times_w(i + 1, 0)
                    if name == "turn_deg":
                        pe.wait_ge(rows_summed, i)
                        if i >= 2:
                            pe.wait_ge(deg1_ready, i - 1)
                        for k in range(TILES):
                            last = nc.tensor.matmul(deg_ps[:, k:k + 1], row_part[:, k * P:(k + 1) * P], ones[:, 0:1],
                                                    start=k == 0, stop=k == TILES - 1)
                        last.then_inc(deg_ready, 1)

            for u in range(PASS2):
                second_unit(PASS1_SPLIT + u)
                scheduled(u)

            def body(layer, slab, chunks, parity=None):
                if isinstance(slab, int):
                    parity = slab % 2
                bank = 1 - parity
                first = isinstance(slab, int) and slab == 0
                n = layer * SLABS + slab - 1
                prev, lay = (LAST, layer) if first else (slab - 1, layer + 1)
                pe.wait_ge(acc_free, evac_index(layer, slab) - 1)
                for u in range(UNITS_PER_SLAB):
                    c = chunks[u // 2]
                    if first and u % 2 == 0:
                        pe.wait_ge(s_lo_ready, layer * SLABS + u // 2 + 1)
                    contract(bank, c, u % 2, u % SPLIT, u == 0, u == UNITS_PER_SLAB - 1, split_index(layer, slab, u))
                    if first and layer == 1:
                        scheduled(PASS2 + u)
                    else:
                        steps_after(after, layer, slab, u)

            for layer in range(1, LAYERS):
                slabs_of(pe, layer, body)
            after(LAYERS * SLABS - 1, LAST, AT["turn_o"], AT, LAYERS)

        @block.gpsimd
        def _(pool):
            nc.gpsimd.memset(ones[:], 1.0).then_inc(pool_consts, 1)
            pool.wait_ge(pool_consts, 1)
            nc.gpsimd.affine_select(out=ident[:], in_=ones[:], compare_op=ALU.is_equal, fill=0.0, base=0,
                                    pattern=[[-1, P]], channel_multiplier=1).then_inc(pool_consts, 1)
            pool.wait_ge(dve_consts, 1)
            pool.wait_ge(bias_step, 2)
            nc.gpsimd.tensor_tensor(bstat[:, 2:3], bstat[:, 1:2], half[:, 0, 0:1], ALU.pow).then_inc(bias_pow, 1)

            def d_step(i):
                pool.wait_ge(deg1_ready, i + 1)
                nc.gpsimd.tensor_tensor(d_of(i), deg1[:], minus_half[:], ALU.pow).then_inc(d_ready, 1)

            def ln_step(p, slab, layer):
                pool.wait_ge(var_ready, p + 1)
                if not isinstance(p, int) or p >= 1:
                    pool.wait_ge(h_ready, p)
                if layer == 2:
                    nc.gpsimd.tensor_tensor(rstd[:], var_eps[:], minus_half[:], ALU.pow).then_inc(rstd_ready, 1)
                    pool.wait_ge(rstd_ready, p - 2 * SLABS + 1)
                    nc.gpsimd.tensor_tensor(ln_scale[:], rstd[:], d_of(slab), ALU.mult).then_inc(scale_ready, 1)
                else:
                    nc.gpsimd.tensor_tensor(ln_scale[:], var_eps[:], minus_half[:], ALU.pow).then_inc(scale_ready, 1)
                pool.wait_ge(scale_ready, p + 1)
                nc.gpsimd.tensor_tensor(ln_bias[:], minus_mean[:], ln_scale[:], ALU.mult).then_inc(ln_ready, 1)

            ln_step(0, 0, 0)
            for i in range(SLABS):
                if i < SLABS - 1:
                    ln_step(i + 1, i + 1, 0)
                if i >= 1:
                    d_step(i - 1)
            d_step(SLABS - 1)
            for t in sorted(SCHEDULE):
                for name, n in SCHEDULE[t]:
                    if name == "stats":
                        ln_step(n + SLABS, LAST - n, 1)
                    if name == "hyp1":
                        w4 = GROUPS[n][1] * TILES
                        pool.wait_ge(hyp_to_pool, 3 * n + 1)
                        nc.gpsimd.tensor_tensor(nrm[:, 0, 0:w4], hyp[:, 4, 0:w4], half[:, 0, 0:w4],
                                                ALU.pow).then_inc(hyp_pow, 1)
                    if name == "hypm":
                        w4 = GROUPS[n][1] * TILES
                        pool.wait_ge(hyp_to_pool, 3 * n + 2)
                        nc.gpsimd.tensor_tensor(nrm[:, 1, 0:w4], hyp[:, 5, 0:w4], half[:, 0, 0:w4],
                                                ALU.pow).then_inc(hyp_pow, 1)
                    if name == "hyp4":
                        w4 = GROUPS[n][1] * TILES
                        pool.wait_ge(hyp_to_pool, 3 * n + 3)
                        nc.gpsimd.tensor_tensor(hyp[:, 18, 0:w4], hyp[:, 17, 0:w4], half[:, 0, 0:w4],
                                                ALU.pow).then_inc(hyp_pow, 1)
            with pool.Fori(0, SLABS) as it:
                pool.wait_ge(relu_ready, it * 2 + 2)
                nc.gpsimd.tensor_tensor(sq[:, 0, :, 0:TILES], sq[:, 0, :, 0:TILES], above_zero[:], ALU.add).then_inc(post_raised, 1)
                pool.wait_ge(post_raised, it + 1)
                nc.gpsimd.tensor_tensor(nrm[:, :, 0:TILES], sq[:, 0, :, 0:TILES], half[:, :, 0:TILES],
                                        ALU.pow).then_inc(hyp_pow, 1)
                ln_step(it + 2 * SLABS, it, 2)
            with pool.Fori(0, SLABS) as it:
                ln_step(it + 3 * SLABS, it, 3)


def kernel(x, adj, L0_gnn_W, L0_gnn_b, L1_gnn_weight, L1_gnn_bias, L2_gnn_W, L2_gnn_b, L3_gnn_weights):
    import numpy as np
    import concourse.bacc as bacc
    from concourse.bass_utils import run_bass_kernel_spmd

    a = np.asarray(adj).reshape(SLABS, SLAB, CHUNKS, 2, 2, P).transpose(0, 2, 3, 5, 4, 1)
    b = np.asarray(adj).reshape(SLABS, 2, 2, P, CHUNKS, SLAB).transpose(0, 4, 1, 3, 2, 5)
    arrays = {
        "adj_units": np.ascontiguousarray(a).reshape(SLABS * CHUNKS * 2 * P, UNIT),
        "adj_row_units": np.ascontiguousarray(b).reshape(SLABS * CHUNKS * 2 * P, UNIT),
        "x_rows": np.ascontiguousarray(np.asarray(x).reshape(N // P, P, F).transpose(1, 0, 2)),
        "weights": np.ascontiguousarray(np.stack([np.asarray(L0_gnn_W), np.asarray(L1_gnn_weight).T,
                                                  np.asarray(L2_gnn_W).T, np.asarray(L3_gnn_weights)], axis=1)),
        "biases": np.ascontiguousarray(np.broadcast_to(
            np.stack([np.asarray(L0_gnn_b), np.asarray(L1_gnn_bias), np.asarray(L2_gnn_b)]), (P, 3, F))),
    }
    nc = bacc.Bacc("TRN2", target_bir_lowering=False, num_devices=1,
                   dynamic_dma_scratch_size=4096)
    aps = [nc.dram_tensor(k, v.shape, FP32, kind="ExternalInput").ap() for k, v in arrays.items()]
    out = nc.dram_tensor("out_rows", (P, N // P, F), FP32, kind="ExternalOutput").ap()
    build(nc, *aps, out)
    r = run_bass_kernel_spmd(nc, [arrays], core_ids=[0])
    got = r.results[0]["out_rows"]
    return np.ascontiguousarray(got.transpose(1, 0, 2)).reshape(N, F)
```
